# Optimizing a Trainium2 kernel written in Bass

```python
import numpy as np
import jax
import jax.numpy as jnp

def _softmax(x, axis=-1):
    return jax.nn.softmax(x, axis=axis)

def _gelu(x):
    return jax.nn.gelu(x, approximate=True)

def _silu(x):
    return jax.nn.silu(x)

def _sigmoid(x):
    return jax.nn.sigmoid(x)

def _layernorm(x, axis=-1, eps=1e-05):
    m = jnp.mean(x, axis=axis, keepdims=True)
    v = jnp.var(x, axis=axis, keepdims=True)
    return (x - m) / jnp.sqrt(v + eps)

def _scatter_add(tgt, idx, src, axis=0):
    return tgt.at[idx].add(src)

def _segment_sum(src, seg, n):
    return jax.ops.segment_sum(src, seg, n)
kernel_name = 'mk_adj_preln_d4_adj_r2_cd3a71'

def setup_inputs(seed: int=0):
    np.random.seed(seed)
    _w = jnp.asarray

    def _rec_inputs():
        import jax
        import jax.numpy as jnp
        _gk = jax.random.key(seed)
        x = -0.0005207 + 1.001 * jax.random.normal(jax.random.fold_in(_gk, 1), (16, 512, 128), jnp.float32)
        _w = (1.0 + jnp.arange(512, dtype=jnp.float32)) ** (-0.5)
        _w = _w / _w.mean()
        _pij = jnp.clip(0.015625 * _w[:, None] * _w[None, :], 0.0, 1.0)
        _a = jax.random.uniform(jax.random.fold_in(_gk, 2), (16, 512, 512)) < _pij
        adj = _a.astype(jnp.int32)
        return (x, adj)
    x, adj = _rec_inputs()

    def _L0_gnn_setup():
        import jax, jax.numpy as jnp
        import numpy as np
        DIM = 128
        HEADS = 4
        B, N = (2, 2048)
        NEG = -1000000000.0
        EPS = 1e-05
        key = jax.random.key(seed)
        ks = jax.random.split(key, 12)
        s = 0.02
        inp = {'x': jax.random.normal(ks[0], (B, N, DIM), dtype=jnp.float32), 'adj': jax.random.randint(ks[1], (B, N, N), 0, 2, dtype=jnp.int32), 'Wq': jax.random.normal(ks[2], (DIM, DIM), dtype=jnp.float32) * s, 'bq': jnp.zeros((DIM,), jnp.float32), 'Wk': jax.random.normal(ks[3], (DIM, DIM), dtype=jnp.float32) * s, 'bk': jnp.zeros((DIM,), jnp.float32), 'Wv': jax.random.normal(ks[4], (DIM, DIM), dtype=jnp.float32) * s, 'bv': jnp.zeros((DIM,), jnp.float32), 'Wo': jax.random.normal(ks[5], (DIM, DIM), dtype=jnp.float32) * s, 'bo': jnp.zeros((DIM,), jnp.float32), 'gamma': jnp.ones((DIM,), jnp.float32), 'beta': jnp.zeros((DIM,), jnp.float32)}
        return inp
    _L0_gnn_all = _L0_gnn_setup()
    _L0_gnn_in = {k: v for k, v in _L0_gnn_all.items() if k in ('Wq', 'bq', 'Wk', 'bk', 'Wv', 'bv', 'Wo', 'bo', 'gamma', 'beta')}
    del _L0_gnn_all

    def _L1_gnn_setup():
        import jax, jax.numpy as jnp
        import numpy as np
        IN_F = 128
        OUT_F = 128
        ALPHA = 0.2

        def _xavier(key, shape, gain=1.414):
            fan_in, fan_out = (shape[0], shape[1])
            limit = gain * np.sqrt(6.0 / (fan_in + fan_out))
            return jax.random.uniform(key, shape, jnp.float32, -limit, limit)
        key = jax.random.key(seed)
        k1, k2, k3, k4 = jax.random.split(key, 4)
        B, N = (8, 1024)
        h = jax.random.normal(k1, (B, N, IN_F), jnp.float32)
        adj = jax.random.randint(k2, (B, N, N), 0, 2, jnp.int32)
        W = _xavier(k3, (IN_F, OUT_F))
        a = _xavier(k4, (2 * OUT_F, 1))
        return {'h': h, 'adj': adj, 'W': W, 'a': a}
    _L1_gnn_all = _L1_gnn_setup()
    _L1_gnn_in = {k: v for k, v in _L1_gnn_all.items() if k in ('W', 'a')}
    del _L1_gnn_all

    def _L2_gnn_setup():
        import jax, jax.numpy as jnp
        import numpy as np
        B, S, D = (64, 256, 128)

        def _leaky(x):
            return jnp.where(x >= 0, x, 0.2 * x)
        key = jax.random.key(seed)
        k = jax.random.split(key, 6)
        stdv = 1.0 / np.sqrt(D)
        return {'hidden': jax.random.normal(k[0], (B, S, D), dtype=jnp.float32), 'adj': jax.random.randint(k[1], (B, S, S), 0, 5, dtype=jnp.int32), 'a0': jax.random.uniform(k[2], (D, 1), jnp.float32, -stdv, stdv), 'a1': jax.random.uniform(k[3], (D, 1), jnp.float32, -stdv, stdv), 'a2': jax.random.uniform(k[4], (D, 1), jnp.float32, -stdv, stdv), 'a3': jax.random.uniform(k[5], (D, 1), jnp.float32, -stdv, stdv), 'bias': jnp.zeros((D,), dtype=jnp.float32)}
    _L2_gnn_all = _L2_gnn_setup()
    _L2_gnn_in = {k: v for k, v in _L2_gnn_all.items() if k in ('a0', 'a1', 'a2', 'a3', 'bias')}
    del _L2_gnn_all

    def _L3_gnn_setup():
        import jax, jax.numpy as jnp
        import numpy as np
        B, N, F_IN, F_OUT = (8, 1024, 128, 128)
        ALPHA = 0.2
        NEG_BIG = -9000000000000000.0
        key = jax.random.key(seed)
        k1, k2, k3, k4 = jax.random.split(key, 4)
        x = jax.random.normal(k1, (B, N, F_IN), dtype=jnp.float32)
        adj = jax.random.randint(k2, (B, N, N), 0, 2, dtype=jnp.int32)
        gain = 1.414
        lim_W = gain * np.sqrt(6.0 / (F_IN + F_OUT))
        W = jax.random.uniform(k3, (F_IN, F_OUT), dtype=jnp.float32, minval=-lim_W, maxval=lim_W)
        lim_a = gain * np.sqrt(6.0 / (2 * F_OUT + 1))
        a = jax.random.uniform(k4, (2 * F_OUT, 1), dtype=jnp.float32, minval=-lim_a, maxval=lim_a)
        return {'x': x, 'adj': adj, 'W': W, 'a': a}
    _L3_gnn_all = _L3_gnn_setup()
    _L3_gnn_in = {k: v for k, v in _L3_gnn_all.items() if k in ('W', 'a')}
    del _L3_gnn_all
    return {'x': x, 'adj': adj, 'L0_gnn_Wq': _L0_gnn_in['Wq'], 'L0_gnn_bq': _L0_gnn_in['bq'], 'L0_gnn_Wk': _L0_gnn_in['Wk'], 'L0_gnn_bk': _L0_gnn_in['bk'], 'L0_gnn_Wv': _L0_gnn_in['Wv'], 'L0_gnn_bv': _L0_gnn_in['bv'], 'L0_gnn_Wo': _L0_gnn_in['Wo'], 'L0_gnn_bo': _L0_gnn_in['bo'], 'L0_gnn_gamma': _L0_gnn_in['gamma'], 'L0_gnn_beta': _L0_gnn_in['beta'], 'L1_gnn_W': _L1_gnn_in['W'], 'L1_gnn_a': _L1_gnn_in['a'], 'L2_gnn_a0': _L2_gnn_in['a0'], 'L2_gnn_a1': _L2_gnn_in['a1'], 'L2_gnn_a2': _L2_gnn_in['a2'], 'L2_gnn_a3': _L2_gnn_in['a3'], 'L2_gnn_bias': _L2_gnn_in['bias'], 'L3_gnn_W': _L3_gnn_in['W'], 'L3_gnn_a': _L3_gnn_in['a']}

def reference(x, adj, L0_gnn_Wq, L0_gnn_bq, L0_gnn_Wk, L0_gnn_bk, L0_gnn_Wv, L0_gnn_bv, L0_gnn_Wo, L0_gnn_bo, L0_gnn_gamma, L0_gnn_beta, L1_gnn_W, L1_gnn_a, L2_gnn_a0, L2_gnn_a1, L2_gnn_a2, L2_gnn_a3, L2_gnn_bias, L3_gnn_W, L3_gnn_a):
    import jax
    import jax.numpy as jnp

    def _L0_gnn_ref(x, adj, Wq, bq, Wk, bk, Wv, bv, Wo, bo, gamma, beta):
        import jax, jax.numpy as jnp
        import numpy as np
        DIM = 128
        HEADS = 4
        B, N = (2, 2048)
        NEG = -1000000000.0
        EPS = 1e-05
        Bx, Nx, C = x.shape
        H = HEADS
        D = C // H
        scale = D ** (-0.5)

        def proj(W, b):
            return (x @ W.T + b).reshape(Bx, Nx, H, D).transpose(0, 2, 1, 3)
        q = proj(Wq, bq)
        k = proj(Wk, bk)
        v = proj(Wv, bv)
        attn = jnp.einsum('bhnd,bhmd->bhnm', q, k) * scale
        attn = jnp.where(adj[:, None, :, :] == 0, NEG, attn)
        attn = jax.nn.softmax(attn, axis=-1)
        out = jnp.einsum('bhnm,bhmd->bhnd', attn, v)
        out = out.transpose(0, 2, 1, 3).reshape(Bx, Nx, C)
        out = out @ Wo.T + bo
        mu = jnp.mean(out, axis=-1, keepdims=True)
        var = jnp.var(out, axis=-1, keepdims=True)
        return (out - mu) * jax.lax.rsqrt(var + EPS) * gamma + beta

    def _L1_gnn_ref(h, adj, W, a):
        import jax, jax.numpy as jnp
        import numpy as np
        IN_F = 128
        OUT_F = 128
        ALPHA = 0.2

        def _xavier(key, shape, gain=1.414):
            fan_in, fan_out = (shape[0], shape[1])
            limit = gain * np.sqrt(6.0 / (fan_in + fan_out))
            return jax.random.uniform(key, shape, jnp.float32, -limit, limit)
        Wh = jnp.einsum('bni,io->bno', h, W)
        a1 = a[:OUT_F, 0]
        a2 = a[OUT_F:, 0]
        e1 = Wh @ a1
        e2 = Wh @ a2
        e = e1[:, :, None] + e2[:, None, :]
        e = jnp.where(e > 0, e, ALPHA * e)
        neg = jnp.float32(-9000000000000000.0)
        scores = jnp.where(adj > 0, e, neg)
        attention = jax.nn.softmax(scores, axis=2)
        h_prime = jnp.einsum('bnm,bmo->bno', attention, Wh)
        return jax.nn.elu(h_prime)

    def _L2_gnn_ref(hidden, adj, a0, a1, a2, a3, bias):
        import jax, jax.numpy as jnp
        import numpy as np
        B, S, D = (64, 256, 128)

        def _leaky(x):
            return jnp.where(x >= 0, x, 0.2 * x)
        h = hidden

        def e_of(a):
            return _leaky(jnp.einsum('bid,bjd->bij', h * a[:, 0], h))
        e0, e1, e2, e3 = (e_of(a0), e_of(a1), e_of(a2), e_of(a3))
        neg_inf = jnp.float32(-jnp.finfo(e0.dtype).max)
        alpha = jnp.where(adj == 1, e0, neg_inf)
        alpha = jnp.where(adj == 2, e1, alpha)
        alpha = jnp.where(adj == 3, e2, alpha)
        alpha = jnp.where(adj == 4, e3, alpha)
        alpha = jax.nn.sigmoid(alpha)
        return jnp.einsum('bij,bjd->bid', alpha, h) + bias

    def _L3_gnn_ref(x, adj, W, a):
        import jax, jax.numpy as jnp
        import numpy as np
        B, N, F_IN, F_OUT = (8, 1024, 128, 128)
        ALPHA = 0.2
        NEG_BIG = -9000000000000000.0
        h = jnp.einsum('bnf,fo->bno', x, W)
        a1 = a[:F_OUT, 0]
        a2 = a[F_OUT:, 0]
        s1 = h @ a1
        s2 = h @ a2
        e = jax.nn.leaky_relu(s1[:, :, None] + s2[:, None, :], negative_slope=ALPHA)
        att = jnp.where(adj > 0, e, jnp.float32(NEG_BIG))
        att = jax.nn.softmax(att, axis=1)
        h_prime = jnp.einsum('bij,bjo->bio', att, h)
        return jax.nn.elu(h_prime)
    h = jnp.maximum(_layernorm(x, axis=-1), 0.0)
    x = x + _L0_gnn_ref(h, adj, L0_gnn_Wq, L0_gnn_bq, L0_gnn_Wk, L0_gnn_bk, L0_gnn_Wv, L0_gnn_bv, L0_gnn_Wo, L0_gnn_bo, L0_gnn_gamma, L0_gnn_beta)
    h = jnp.maximum(_layernorm(x, axis=-1), 0.0)
    x = x + _L1_gnn_ref(h, adj, L1_gnn_W, L1_gnn_a)
    h = jnp.maximum(_layernorm(x, axis=-1), 0.0)
    x = x + _L2_gnn_ref(h, adj, L2_gnn_a0, L2_gnn_a1, L2_gnn_a2, L2_gnn_a3, L2_gnn_bias)
    h = jnp.maximum(_layernorm(x, axis=-1), 0.0)
    x = x + _L3_gnn_ref(h, adj, L3_gnn_W, L3_gnn_a)
    return x

_drawn_inputs = setup_inputs


def setup_inputs(seed=0):
    import zlib

    import numpy as np

    out = dict(_drawn_inputs(seed))
    spreads = {'L0_gnn_bq': (0.0, 2.0),
     'L0_gnn_bk': (0.0, 2.0),
     'L0_gnn_bv': (0.0, 0.1),
     'L0_gnn_bo': (0.0, 0.1),
     'L0_gnn_gamma': (1.0, 0.2),
     'L0_gnn_beta': (0.0, 0.1),
     'L2_gnn_bias': (0.0, 0.359)}
    factors = {'L0_gnn_Wq': 8.0, 'L0_gnn_Wk': 8.0}
    for name, (base, spread) in spreads.items():
        noise = np.random.default_rng([zlib.crc32(name.encode()), seed]).standard_normal(out[name].shape)
        drawn = base * np.exp(spread * noise) if base else spread * noise
        out[name] = jnp.asarray(drawn.astype(out[name].dtype))
    for name, factor in factors.items():
        out[name] = (out[name] * factor).astype(out[name].dtype)
    return out
```

```python
from contextlib import ExitStack

import numpy as np

import concourse.bass as bass
from concourse import mybir

F32 = mybir.dt.float32
F32R = mybir.dt.float32r
BF16 = mybir.dt.bfloat16
U16 = mybir.dt.uint16
ALU = mybir.AluOpType
ACT = mybir.ActivationFunctionType

P = 128
BATCH, NODES, DIM = 16, 512, 128
TILES = NODES // P
HEADS = 4
HDIM = DIM // HEADS
ROW = TILES * DIM
PAIRS = BATCH // 2
EPS = 1e-05
BIG = 2.0 ** 100
FAR = 3.0e38
SLOPE = 0.2


def due(count):
    return not isinstance(count, int) or count > 0


def held(eng, count):
    return count if isinstance(count, int) else eng.to_reg(count)


def over_batches(eng, body):
    for par in range(2):
        body(0, par, True, True)
    with eng.Fori(1, PAIRS - 1) as i:
        for par in range(2):
            body(i, par, True, True)
    for par in range(2):
        body(PAIRS - 1, par, par == 0, False)


class Build:

    def __init__(self, nc, ctx, layer):
        self.nc, self.ctx, self.layer = nc, ctx, layer

    def sb(self, name, shape, dt=F32):
        return self.ctx.enter_context(self.nc.sbuf_tensor(f"{self.layer}_{name}", shape, dt))

    def ps(self, name, shape, dt=F32):
        return self.ctx.enter_context(self.nc.psum_tensor(f"{self.layer}_{name}", shape, dt))

    def sem(self, name):
        return self.ctx.enter_context(self.nc.semaphore(f"{self.layer}_{name}"))


class Norm:

    def __init__(self, k, name, c):
        self.parts = k.sb(f"{name}_parts", [P, TILES, 6])
        self.mv = k.sb(f"{name}_mv", [P, TILES, 2])
        self.var = k.sb(f"{name}_var", [P, TILES])
        self.rstd = k.sb(f"{name}_rstd", [P, TILES])
        self.mr = k.sb(f"{name}_mr", [P, TILES])
        self.shift = k.sb(f"{name}_shift", [P, TILES])
        self.parts_done = k.sem(f"{name}_parts_done")
        self.moments = k.sem(f"{name}_moments")
        self.var_done = k.sem(f"{name}_var_done")
        self.rstd_done = k.sem(f"{name}_rstd_done")
        self.mr_done = k.sem(f"{name}_mr_done")
        self.ready = k.sem(f"{name}_ready")
        self.c = c

    def on_dve(self, nc, dve, tile, n):
        if due(n):
            dve.wait_ge(self.mr_done, n)
        for t in range(TILES):
            last = nc.vector.bn_stats(self.parts[:, t, :], tile(t))
        last.then_inc(self.parts_done, 1)
        count = held(dve, n + 1)
        dve.wait_ge(self.parts_done, 1)
        dve.wait_ge(self.parts_done, count)
        for t in range(TILES):
            last = nc.vector.bn_aggr(self.mv[:, t, :], self.parts[:, t, :])
        last.then_inc(self.moments, 1)

    def on_pool(self, nc, pool, n, used, used_count):
        count = held(pool, n + 1)
        pool.wait_ge(self.moments, 1)
        pool.wait_ge(self.moments, count)
        nc.gpsimd.tensor_scalar(self.var[:], self.mv[:, :, 1], EPS, 1.0, ALU.add, ALU.mult).then_inc(self.var_done, 1)
        pool.wait_ge(self.var_done, n + 1)
        if due(used_count):
            pool.wait_ge(used, used_count)
        nc.gpsimd.tensor_tensor(self.rstd[:], self.var[:], self.c["minus_half"][:], ALU.pow).then_inc(self.rstd_done, 1)
        pool.wait_ge(self.rstd_done, n + 1)
        nc.gpsimd.tensor_tensor(self.mr[:], self.mv[:, :, 0], self.rstd[:], ALU.mult).then_inc(self.mr_done, 1)
        count = held(pool, n + 1)
        pool.wait_ge(self.mr_done, 1)
        pool.wait_ge(self.mr_done, count)
        nc.gpsimd.tensor_scalar(self.shift[:], self.mr[:], -1.0, 1.0, ALU.mult, ALU.mult).then_inc(self.ready, 1)

    def apply(self, nc, act, out, tile, n, func):
        act.wait_ge(self.ready, n + 1)
        for t in range(TILES):
            last = nc.scalar.activation(out[:, t * DIM:(t + 1) * DIM], tile(t), func,
                                        bias=self.shift[:, t:t + 1], scale=self.rstd[:, t:t + 1])
        return last


def layer0(nc, c, X, x_in, adj_in, w):
    with ExitStack() as ctx:
        k = Build(nc, ctx, "att")
        norm, post = Norm(k, "norm", c), Norm(k, "post", c)
        adj = k.sb("adj", [P, 2, TILES * NODES], BF16)
        away = k.sb("away", [P, 2, TILES * NODES], BF16)
        h = k.sb("h", [P, ROW])
        hT = k.sb("hT", [P, NODES])
        qhi, qlo = k.sb("qhi", [P, NODES], F32R), k.sb("qlo", [P, NODES], F32R)
        khi, klo = k.sb("khi", [P, NODES], F32R), k.sb("klo", [P, NODES], F32R)
        qs = k.sb("qs", [3 * HDIM, 2, HEADS, NODES], F32R)
        ks = k.sb("ks", [3 * HDIM, 2, HEADS, NODES], F32R)
        V = k.sb("v", [P, 2, TILES * DIM])
        score = k.sb("score", [P, HEADS, NODES])
        low = k.sb("low", [P, HEADS])
        prob = k.sb("prob", [P, 2, HEADS, NODES])
        total = k.sb("total", [P, 2, HEADS])
        rtotal = k.sb("rtotal", [P, 2, HEADS])
        probT = k.sb("probT", [P, 2, TILES, HEADS, 2 * P])
        oT = k.sb("oT", [P, NODES])
        y = k.sb("y", [P, ROW])
        yn = k.sb("yn", [P, ROW])
        yg = k.sb("yg", [P, ROW])
        yb = k.sb("yb", [P, ROW])

        psS = k.ps("psS", [P, HEADS, NODES])
        psT = k.ps("psT", [P, 2, TILES, P])
        psO = k.ps("psO", [P, NODES])
        psW = k.ps("psW", [P, NODES])

        x_got = [k.sem(f"x_got{i}") for i in range(2)]
        adj_got = [k.sem(f"adj_got{i}") for i in range(2)]
        stacked = [k.sem(f"stacked{i}") for i in range(2)]
        names = ("masked h_ready hT_psum hT_ready q_psum qhi_ready qlo_ready k_psum khi_ready klo_ready v_psum "
                 "v_ready score_psum score_ready exp_ready rtotal_ready prob_ready probT_psum probT_act probT_dve "
                 "pv_done oT_ready proj_psum y_ready yn_ready yg_ready yb_ready x_updated")
        s = {n: k.sem(n) for n in names.split()}
        block = ctx.enter_context(nc.Block())

        def x_tile(b):
            return lambda t: X[:, bass.ds(b * ROW + t * DIM, DIM)]

        @block.sync
        def _(sp):
            def load_x(i, par):
                sp.dma_start(X[:, bass.ds((2 * i + par) * ROW, ROW)].rearrange("p (t c) -> p t c", c=DIM),
                             x_in[bass.ds(2 * i + par, 1), :, :].rearrange("b (t p) c -> p (b t) c", p=P)
                             ).then_inc(x_got[par], 16)

            def restack(i, par, n):
                count = held(sp, 16 * (n - 1))
                if due(count):
                    sp.wait_ge(s["score_psum"], 1)
                    sp.wait_ge(s["score_psum"], count)
                for hi_, lo_, dst, parts in (("qhi_ready", "qlo_ready", qs, (qhi, qhi, qlo)),
                                             ("khi_ready", "klo_ready", ks, (khi, klo, khi))):
                    count, count_2 = held(sp, n + 1), held(sp, n + 1)
                    sp.wait_ge(s[hi_], 1)
                    sp.wait_ge(s[hi_], count)
                    sp.wait_ge(s[lo_], count_2)
                    for r, src in enumerate(parts):
                        for hd in range(HEADS):
                            sp.dma_start(dst[r * HDIM:(r + 1) * HDIM, par, hd, :].bitcast(F32),
                                         src[hd * HDIM:(hd + 1) * HDIM, :].bitcast(F32)).then_inc(stacked[par], 16)

            load_x(0, 0)
            load_x(0, 1)
            restack(0, 0, 0)

            def body(i, par, more, more2):
                if more2:
                    load_x(i + 1, par)
                if more:
                    restack(i + par, 1 - par, 2 * i + par + 1)
            over_batches(sp, body)

        @block.gpsimd
        def _(pool):
            def load_adj(i, par):
                b = 2 * i + par
                if due(b - 1):
                    pool.wait_ge(s["masked"], b - 1)
                pool.dma_start(adj[:, par, :].rearrange("p (t m) -> p t m", m=NODES),
                               adj_in[bass.ds(b, 1), :, :].rearrange("b (t p) m -> p (b t) m", p=P)
                               ).then_inc(adj_got[par], 16)

            load_adj(0, 0)
            load_adj(0, 1)
            norm.on_pool(nc, pool, 0, s["h_ready"], 0)

            def finish(b):
                pool.wait_ge(s["yn_ready"], b + 1)
                nc.gpsimd.tensor_tensor(yg[:], yn[:], c["gamma"][:], ALU.mult).then_inc(s["yg_ready"], 1)
                pool.wait_ge(s["yg_ready"], b + 1)
                nc.gpsimd.tensor_tensor(yb[:], yg[:], c["beta"][:], ALU.add).then_inc(s["yb_ready"], 1)
                pool.wait_ge(s["yb_ready"], b + 1)
                xb = X[:, bass.ds(b * ROW, ROW)]
                nc.gpsimd.tensor_tensor(xb, xb, yb[:], ALU.add).then_inc(s["x_updated"], 1)

            def body(i, par, more, more2):
                b = 2 * i + par
                first = isinstance(b, int) and b == 0
                if more2:
                    load_adj(i + 1, par)
                for nt in range(TILES):
                    g = 4 * b + nt
                    pool.wait_ge(s["exp_ready"], 4 * g + 4)
                    nc.gpsimd.tensor_tensor(rtotal[:, nt % 2, :], total[:, nt % 2, :], c["minus_one"][:],
                                            ALU.pow).then_inc(s["rtotal_ready"], 1)
                    count = held(pool, g + 1)
                    pool.wait_ge(s["rtotal_ready"], 1)
                    pool.wait_ge(s["rtotal_ready"], count)
                    for hd in range(HEADS):
                        pr = prob[:, nt % 2, hd, :]
                        nc.gpsimd.tensor_scalar(pr, pr, rtotal[:, nt % 2, hd:hd + 1], 1.0,
                                                ALU.mult, ALU.mult).then_inc(s["prob_ready"], 1)
                    if nt == 0 and more:
                        norm.on_pool(nc, pool, b + 1, s["h_ready"], b + 1)
                    if nt == 1 and not first:
                        post.on_pool(nc, pool, b - 1, s["yn_ready"], b - 1)
                    if nt == 2 and not first:
                        finish(b - 1)
            over_batches(pool, body)
            post.on_pool(nc, pool, BATCH - 1, s["yn_ready"], BATCH - 1)
            finish(BATCH - 1)

        @block.vector
        def _(dve):
            def mask(i, par, n):
                dve.wait_ge(adj_got[par], 16 * (i + 1))
                nc.vector.tensor_scalar(away[:, par, :], adj[:, par, :], 0.0, BIG, ALU.is_equal,
                                        ALU.mult).then_inc(s["masked"], 1)

            def low_half(name, ps_sem, hi_, lo_, bias, par_before, n):
                dve.wait_ge(s[f"{name}hi_ready"], n + 1)
                if par_before is not None:
                    i_b, p_b = par_before
                    dve.wait_ge(stacked[p_b], 16 * 6 * HEADS * (i_b + 1))
                nc.vector.scalar_tensor_tensor(out=lo_[:], in0=psW[:], scalar=bias, in1=hi_[:],
                                               op0=ALU.add, op1=ALU.subtract).then_inc(s[f"{name}lo_ready"], 1)

            def value(par, n):
                dve.wait_ge(s["v_psum"], n + 1)
                if due(2 * (n - 1)):
                    dve.wait_ge(s["pv_done"], 2 * (n - 1))
                nc.vector.tensor_tensor(V[:, par, :], psW[:], c["bv"][:], ALU.add).then_inc(s["v_ready"], 1)

            def masked_scores(b, par, nt, hd):
                g = 4 * b + nt
                count, count_2 = held(dve, 4 * g + hd + 1), held(dve, 4 * (g - 1) + hd + 1)
                dve.wait_ge(s["score_psum"], 1)
                dve.wait_ge(s["score_psum"], count)
                if due(count_2):
                    dve.wait_ge(s["exp_ready"], count_2)
                nc.vector.tensor_tensor_reduce(score[:, hd, :], psS[:, hd, :],
                                               away[:, par, nt * NODES:(nt + 1) * NODES], 1.0, FAR,
                                               ALU.add, ALU.min, low[:, hd:hd + 1]).then_inc(s["score_ready"], 1)

            def evacuate(b, nt, hd):
                g = 4 * b + nt
                dve.wait_ge(s["probT_psum"], 4 * g + hd + 1)
                if due(2 * b + nt // 2 - 1):
                    dve.wait_ge(s["pv_done"], 2 * b + nt // 2 - 1)
                nc.vector.tensor_copy(probT[:, nt // 2, :, hd, (nt % 2) * P:(nt % 2 + 1) * P],
                                      psT[:, hd % 2, :, :]).then_inc(s["probT_dve"], 1)

            def project(n):
                dve.wait_ge(s["proj_psum"], n + 1)
                if due(n):
                    dve.wait_ge(s["yn_ready"], n)
                nc.vector.tensor_tensor(y[:], psW[:], c["bo"][:], ALU.add).then_inc(s["y_ready"], 1)
                dve.wait_ge(s["y_ready"], n + 1)
                post.on_dve(nc, dve, lambda t: y[:, t * DIM:(t + 1) * DIM], n)

            def statistics(i, par, b):
                dve.wait_ge(x_got[par], 16 * (i + 1))
                norm.on_dve(nc, dve, x_tile(b), b)

            statistics(0, 0, 0)
            mask(0, 0, 0)
            low_half("q", None, qhi, qlo, w["bqs"][:, 0:1], None, 0)
            low_half("k", None, khi, klo, w["bk"][:, 0:1], None, 0)
            value(0, 0)
            dve.wait_ge(s["masked"], 1)
            for hd in range(HEADS):
                masked_scores(0, 0, 0, hd)

            def body(i, par, more, more2):
                b = 2 * i + par
                first = isinstance(b, int) and b == 0
                if more:
                    statistics(i + par, 1 - par, b + 1)
                for nt in range(TILES):
                    if nt == 3:
                        evacuate(b, nt, 1)
                        evacuate(b, nt, 3)
                        if more:
                            dve.wait_ge(s["masked"], b + 2)
                            for hd in range(HEADS):
                                masked_scores(b + 1, 1 - par, 0, hd)
                        continue
                    masked_scores(b, par, nt + 1, 0)
                    masked_scores(b, par, nt + 1, 1)
                    evacuate(b, nt, 1)
                    masked_scores(b, par, nt + 1, 2)
                    evacuate(b, nt, 3)
                    masked_scores(b, par, nt + 1, 3)
                    if nt == 0 and not first:
                        project(b - 1)
                    if nt == 0 and more:
                        mask(i + par, 1 - par, b + 1)
                    if nt == 1 and more:
                        low_half("q", None, qhi, qlo, w["bqs"][:, 0:1], (i, par), b + 1)
                    if nt == 2 and more:
                        low_half("k", None, khi, klo, w["bk"][:, 0:1], (i, par), b + 1)
                        value(1 - par, b + 1)
            over_batches(dve, body)
            project(BATCH - 1)

        @block.scalar
        def _(act):
            def hidden(b, n):
                if due(n):
                    act.wait_ge(s["hT_psum"], n)
                norm.apply(nc, act, h, x_tile(b), n, ACT.Relu).then_inc(s["h_ready"], 1)

            def hidden_T(n):
                act.wait_ge(s["hT_psum"], n + 1)
                if due(n):
                    act.wait_ge(s["v_psum"], n)
                nc.scalar.activation(hT[:], psW[:], ACT.Copy).then_inc(s["hT_ready"], 1)

            def high_half(name, hi_, bias, par_before, n):
                act.wait_ge(s[f"{name}_psum"], n + 1)
                if par_before is not None:
                    i_b, p_b = par_before
                    act.wait_ge(stacked[p_b], 16 * 6 * HEADS * (i_b + 1))
                nc.scalar.activation(hi_[:], psW[:], ACT.Identity, bias=bias).then_inc(s[f"{name}hi_ready"], 1)

            def exponentials(b, nt, par_g, hd):
                g = 4 * b + nt
                act.wait_ge(s["score_ready"], 4 * g + hd + 1)
                if due(4 * (g - 2) + hd + 1):
                    act.wait_ge(s["probT_psum"], 4 * (g - 2) + hd + 1)
                nc.scalar.activation(prob[:, par_g, hd, :], score[:, hd, :], ACT.Exp, bias=low[:, hd:hd + 1],
                                     scale=-1.0, accum_out=total[:, par_g, hd:hd + 1]).then_inc(s["exp_ready"], 1)

            def evacuate(b, nt, hd):
                g = 4 * b + nt
                act.wait_ge(s["probT_psum"], 4 * g + hd + 1)
                if due(2 * b + nt // 2 - 1):
                    act.wait_ge(s["pv_done"], 2 * b + nt // 2 - 1)
                nc.scalar.activation(probT[:, nt // 2, :, hd, (nt % 2) * P:(nt % 2 + 1) * P],
                                     psT[:, hd % 2, :, :], ACT.Copy).then_inc(s["probT_act"], 1)

            def outputs_T(n):
                act.wait_ge(s["pv_done"], 2 * n + 2)
                if due(n):
                    act.wait_ge(s["proj_psum"], n)
                nc.scalar.activation(oT[:], psO[:], ACT.Copy).then_inc(s["oT_ready"], 1)

            def normalise(n):
                if due(n):
                    act.wait_ge(s["yg_ready"], n)
                post.apply(nc, act, yn, lambda t: y[:, t * DIM:(t + 1) * DIM], n, ACT.Identity).then_inc(s["yn_ready"], 1)

            hidden(0, 0)
            hidden_T(0)
            high_half("q", qhi, w["bqs"][:, 0:1], None, 0)
            high_half("k", khi, w["bk"][:, 0:1], None, 0)
            for hd in range(HEADS):
                exponentials(0, 0, 0, hd)

            def body(i, par, more, more2):
                b = 2 * i + par
                first = isinstance(b, int) and b == 0
                for nt in range(TILES):
                    if nt == 3:
                        evacuate(b, nt, 0)
                        evacuate(b, nt, 2)
                        if more:
                            for hd in range(HEADS):
                                exponentials(b + 1, 0, 0, hd)
                        continue
                    exponentials(b, nt + 1, (nt + 1) % 2, 0)
                    if nt == 0 and not first:
                        outputs_T(b - 1)
                    evacuate(b, nt, 0)
                    exponentials(b, nt + 1, (nt + 1) % 2, 1)
                    evacuate(b, nt, 2)
                    if nt == 1 and more:
                        hidden_T(b + 1)
                    exponentials(b, nt + 1, (nt + 1) % 2, 2)
                    exponentials(b, nt + 1, (nt + 1) % 2, 3)
                    if nt == 0 and more:
                        hidden(b + 1, b + 1)
                    if nt == 1 and more:
                        high_half("q", qhi, w["bqs"][:, 0:1], (i, par), b + 1)
                    if nt == 1 and not first:
                        normalise(b - 1)
                    if nt == 2 and more:
                        high_half("k", khi, w["bk"][:, 0:1], (i, par), b + 1)
            over_batches(act, body)
            outputs_T(BATCH - 1)
            normalise(BATCH - 1)

        @block.tensor
        def _(pe):
            def transpose_h(n, before, before_count):
                pe.wait_ge(s["h_ready"], n + 1)
                if due(before_count):
                    pe.wait_ge(before, before_count)
                for t in range(TILES):
                    last = nc.tensor.transpose(psW[:, t * P:(t + 1) * P], h[:, t * DIM:(t + 1) * DIM], c["ident"][:])
                last.then_inc(s["hT_psum"], 1)

            def query(n):
                pe.wait_ge(s["hT_ready"], n + 1)
                nc.tensor.matmul(psW[:], w["wqT"][:], hT[:], start=True, stop=True).then_inc(s["q_psum"], 1)

            def key(n):
                pe.wait_ge(s["qlo_ready"], n + 1)
                nc.tensor.matmul(psW[:], w["wkT"][:], hT[:], start=True, stop=True).then_inc(s["k_psum"], 1)

            def value(n):
                pe.wait_ge(s["klo_ready"], n + 1)
                for t in range(TILES):
                    last = nc.tensor.matmul(psW[:, t * DIM:(t + 1) * DIM], hT[:, t * P:(t + 1) * P], w["wvT"][:],
                                            start=True, stop=True)
                last.then_inc(s["v_psum"], 1)

            def scores(i, par, b, nt):
                g = 4 * b + nt
                pe.wait_ge(stacked[par], 16 * 6 * HEADS * (i + 1))
                for hd in range(HEADS):
                    if due(4 * (g - 1) + hd + 1):
                        pe.wait_ge(s["score_ready"], 4 * (g - 1) + hd + 1)
                    nc.tensor.matmul(psS[:, hd, :], qs[:, par, hd, nt * P:(nt + 1) * P], ks[:, par, hd, :],
                                     start=True, stop=True).then_inc(s["score_psum"], 1)

            def transpose_probs(b, nt):
                g = 4 * b + nt
                for hd in range(HEADS):
                    pe.wait_ge(s["prob_ready"], 4 * g + hd + 1)
                    if due(2 * g + hd // 2):
                        pe.wait_ge(s["probT_act" if hd % 2 == 0 else "probT_dve"], 2 * g + hd // 2)
                    for mt in range(TILES):
                        last = nc.tensor.transpose(psT[:, hd % 2, mt, :], prob[:, nt % 2, hd, mt * P:(mt + 1) * P],
                                                   c["ident"][:])
                    last.then_inc(s["probT_psum"], 1)

            def weigh(b, par, half):
                pe.wait_ge(s["v_ready"], b + 1)
                pe.wait_ge(s["probT_act"], 8 * b + 4 * half + 4)
                pe.wait_ge(s["probT_dve"], 8 * b + 4 * half + 4)
                if half == 0:
                    if due(b):
                        pe.wait_ge(s["oT_ready"], b)
                for mt in range(TILES):
                    for hd in range(HEADS):
                        last = nc.tensor.matmul(psO[hd * HDIM:(hd + 1) * HDIM, half * 2 * P:(half + 1) * 2 * P],
                                                V[:, par, mt * DIM + hd * HDIM:mt * DIM + (hd + 1) * HDIM],
                                                probT[:, half, mt, hd, :], start=(mt == 0), stop=(mt == TILES - 1),
                                                skip_group_check=True)
                last.then_inc(s["pv_done"], 1)

            def project(n):
                pe.wait_ge(s["oT_ready"], n + 1)
                for t in range(TILES):
                    last = nc.tensor.matmul(psW[:, t * DIM:(t + 1) * DIM], oT[:, t * P:(t + 1) * P], w["woT"][:],
                                            start=True, stop=True)
                last.then_inc(s["proj_psum"], 1)

            transpose_h(0, s["h_ready"], 1)
            query(0)
            key(0)
            value(0)
            scores(0, 0, 0, 0)

            def body(i, par, more, more2):
                b = 2 * i + par
                first = isinstance(b, int) and b == 0
                scores(i, par, b, 1)
                if not first:
                    weigh(b - 1, 1 - par, 1)
                transpose_probs(b, 0)
                if not first:
                    pe.wait_ge(s["v_ready"], b + 1)
                    project(b - 1)
                scores(i, par, b, 2)
                if more:
                    if first:
                        transpose_h(1, s["v_ready"], 1)
                    else:
                        transpose_h(b + 1, s["y_ready"], b)
                transpose_probs(b, 1)
                if more:
                    query(b + 1)
                scores(i, par, b, 3)
                weigh(b, par, 0)
                if more:
                    key(b + 1)
                transpose_probs(b, 2)
                if more:
                    value(b + 1)
                transpose_probs(b, 3)
                if more:
                    scores(i + par, 1 - par, b + 1, 0)
            over_batches(pe, body)
            weigh(BATCH - 1, 1, 1)
            pe.wait_ge(s["v_ready"], BATCH)
            project(BATCH - 1)


def graph_attention(nc, c, X, adj_in, w, codes, out, last_layer):
    with ExitStack() as ctx:
        k = Build(nc, ctx, "gat3" if last_layer else "gat1")
        norm = Norm(k, "norm", c)
        if not last_layer:
            adj = k.sb("adj", [P, 2, TILES * NODES], BF16)
        away = k.sb("away", [P, 2, TILES * NODES], BF16)
        h = k.sb("h", [P, ROW])
        hT = k.sb("hT", [P, NODES])
        wh = k.sb("wh", [P, 2, ROW])
        whs = k.sb("whs", [P, 2, ROW])
        e_own = k.sb("e_own", [P, 2, TILES])
        e_row = k.sb("e_row", [P, 2, NODES])
        rise = k.sb("rise", [P, TILES, NODES])
        base = k.sb("base", [P, TILES, NODES])
        score = k.sb("score", [P, 4, NODES])
        top = k.sb("top", [P, 4])
        ntop = k.sb("ntop", [P, 4])
        prob = k.sb("prob", [P, 2, TILES, NODES])
        total = k.sb("total", [P, 2, TILES])
        rtotal = k.sb("rtotal", [P, 2, TILES])
        probT = k.sb("probT", [P, 2, TILES, NODES])
        neg = k.sb("neg", [P, ROW])
        pos = k.sb("pos", [P, ROW])
        expneg = k.sb("expneg", [P, ROW])

        psW = k.ps("psW", [P, NODES])
        psE = k.ps("psE", [P, NODES])
        psR = k.ps("psR", [P, NODES])
        psO = k.ps("psO", [P, NODES])
        psT = k.ps("psT", [P, 2, TILES, P])

        adj_got = [k.sem(f"adj_got{i}") for i in range(2)]
        names = ("masked h_ready hT_psum hT_ready wh_psum wh_ready eown_psum eown_ready erow_psum erow_ready "
                 "rise_ready base_ready score_ready ntop_ready exp_ready rtotal_ready prob_ready probT_psum probT_act probT_dve "
                 "pv_done neg_ready pos_ready expneg_ready x_updated")
        s = {n: k.sem(n) for n in names.split()}
        stored = [k.sem(f"stored{i}") for i in range(2)]
        block = ctx.enter_context(nc.Block())

        def x_tile(b):
            return lambda t: X[:, bass.ds(b * ROW + t * DIM, DIM)]

        if last_layer:
            @block.sync
            def _(sp):
                def body(i, par, more, more2):
                    b = 2 * i + par
                    count = held(sp, b + 1)
                    sp.wait_ge(s["x_updated"], 1)
                    sp.wait_ge(s["x_updated"], count)
                    sp.dma_start(out[bass.ds(b, 1), :, :].rearrange("b (t p) c -> p (b t) c", p=P),
                                 X[:, bass.ds(b * ROW, ROW)].rearrange("p (t c) -> p t c", c=DIM)
                                 ).then_inc(stored[par], 16)
                over_batches(sp, body)
                for par in range(2):
                    sp.wait_ge(stored[par], 16 * PAIRS)

        @block.gpsimd
        def _(pool):
            def load_adj(i, par):
                b = 2 * i + par
                if due(b - 1):
                    pool.wait_ge(s["masked"], b - 1)
                pool.dma_start(adj[:, par, :].rearrange("p (t m) -> p t m", m=NODES),
                               adj_in[bass.ds(b, 1), :, :].rearrange("b (t p) m -> p (b t) m", p=P)
                               ).then_inc(adj_got[par], 16)

            def bases(b, par):
                pool.wait_ge(s["masked"], b + 1)
                pool.wait_ge(s["erow_ready"], b + 1)
                for t in range(TILES):
                    if due(4 * b + t - 3):
                        pool.wait_ge(s["score_ready"], 4 * b + t - 3)
                    nc.gpsimd.tensor_tensor(base[:, t, :], away[:, par, t * NODES:(t + 1) * NODES], e_row[:, par, :],
                                            ALU.add).then_inc(s["base_ready"], 1)

            if not last_layer:
                load_adj(0, 0)
                load_adj(0, 1)
            norm.on_pool(nc, pool, 0, s["h_ready"], 0)
            bases(0, 0)

            def body(i, par, more, more2):
                b = 2 * i + par
                if more2 and not last_layer:
                    load_adj(i + 1, par)
                if more:
                    norm.on_pool(nc, pool, b + 1, s["h_ready"], b + 1)
                pool.wait_ge(s["exp_ready"], 4 * b + 4)
                nc.gpsimd.tensor_tensor(rtotal[:, par, :], total[:, par, :], c["minus_one"][:],
                                        ALU.pow).then_inc(s["rtotal_ready"], 1)
                if last_layer:
                    count, count_2, count_3 = held(pool, b + 1), held(pool, b + 1), held(pool, b - 1)
                    pool.wait_ge(s["rtotal_ready"], 1)
                    pool.wait_ge(s["rtotal_ready"], count)
                    pool.wait_ge(s["wh_ready"], count_2)
                    if due(count_3):
                        pool.wait_ge(s["pv_done"], count_3)
                else:
                    count = held(pool, b + 1)
                    pool.wait_ge(s["rtotal_ready"], 1)
                    pool.wait_ge(s["rtotal_ready"], count)
                for t in range(TILES):
                    if last_layer:
                        nc.gpsimd.tensor_scalar(whs[:, par, t * DIM:(t + 1) * DIM], wh[:, par, t * DIM:(t + 1) * DIM],
                                                rtotal[:, par, t:t + 1], 1.0, ALU.mult,
                                                ALU.mult).then_inc(s["prob_ready"], 1)
                    else:
                        nc.gpsimd.tensor_scalar(prob[:, par, t, :], prob[:, par, t, :], rtotal[:, par, t:t + 1], 1.0,
                                                ALU.mult, ALU.mult).then_inc(s["prob_ready"], 1)
                if more:
                    bases(b + 1, 1 - par)
            over_batches(pool, body)

        @block.vector
        def _(dve):
            def front(i, par, b):
                norm.on_dve(nc, dve, x_tile(b), b)
                if last_layer:
                    src = codes[:, bass.ds(b * TILES * NODES, TILES * NODES)]
                else:
                    dve.wait_ge(adj_got[par], 16 * (i + 1))
                    src = adj[:, par, :]
                if due(4 * (b - 1)):
                    dve.wait_ge(s["base_ready"], 4 * (b - 1))
                nc.vector.tensor_scalar(away[:, par, :], src, 0.0, -BIG, ALU.is_le,
                                        ALU.mult).then_inc(s["masked"], 1)

            def front_psum(par, b):
                dve.wait_ge(s["wh_psum"], b + 1)
                if due(b - 1):
                    dve.wait_ge(s["pv_done"], b - 1)
                nc.vector.tensor_copy(wh[:, par, :], psW[:]).then_inc(s["wh_ready"], 1)
                dve.wait_ge(s["eown_psum"], b + 1)
                if due(4 * (b - 1)):
                    dve.wait_ge(s["rise_ready"], 4 * (b - 1))
                nc.vector.tensor_scalar(e_own[:, par, :], psE[:, 0:TILES], 1.0 - SLOPE, None,
                                        ALU.mult).then_inc(s["eown_ready"], 1)

            def masked_scores(b, par, t):
                u = 4 * b + t
                count, count_2, count_3 = held(dve, u + 1), held(dve, u + 1), held(dve, u - 3)
                dve.wait_ge(s["rise_ready"], 1)
                dve.wait_ge(s["rise_ready"], count)
                dve.wait_ge(s["base_ready"], count_2)
                if due(count_3):
                    dve.wait_ge(s["exp_ready"], count_3)
                nc.vector.tensor_tensor_reduce(score[:, t, :], rise[:, t, :], base[:, t, :], 1.0, -FAR,
                                               ALU.add, ALU.max, top[:, t:t + 1]).then_inc(s["score_ready"], 1)
                dve.wait_ge(s["score_ready"], u + 1)
                nc.vector.tensor_scalar(ntop[:, t:t + 1], top[:, t:t + 1], -1.0, None,
                                        ALU.mult).then_inc(s["ntop_ready"], 1)

            def evacuate(b, par, t):
                dve.wait_ge(s["probT_psum"], 4 * b + t + 1)
                if due(b - 1):
                    dve.wait_ge(s["pv_done"], b - 1)
                nc.vector.tensor_copy(probT[:, par, :, t * P:(t + 1) * P], psT[:, t % 2, :, :]
                                      ).then_inc(s["probT_dve"], 1)

            def split(n):
                dve.wait_ge(s["pv_done"], n + 1)
                if due(n):
                    dve.wait_ge(s["expneg_ready"], n)
                nc.vector.tensor_scalar(neg[:], psO[:], 0.0, None, ALU.min).then_inc(s["neg_ready"], 1)
                xb = X[:, bass.ds(n * ROW, ROW)]
                if due(n):
                    dve.wait_ge(s["x_updated"], n)
                nc.vector.scalar_tensor_tensor(out=pos[:], in0=psO[:], scalar=0.0, in1=xb,
                                               op0=ALU.max, op1=ALU.add).then_inc(s["pos_ready"], 1)

            def update(n):
                dve.wait_ge(s["expneg_ready"], n + 1)
                dve.wait_ge(s["pos_ready"], n + 1)
                xb = X[:, bass.ds(n * ROW, ROW)]
                nc.vector.scalar_tensor_tensor(out=xb, in0=expneg[:], scalar=-1.0, in1=pos[:],
                                               op0=ALU.add, op1=ALU.add).then_inc(s["x_updated"], 1)

            front(0, 0, 0)
            front_psum(0, 0)
            for t in range(TILES):
                masked_scores(0, 0, t)

            def body(i, par, more, more2):
                b = 2 * i + par
                if more:
                    front(i + par, 1 - par, b + 1)
                    front_psum(1 - par, b + 1)
                if not last_layer:
                    evacuate(b, par, 1)
                if more:
                    masked_scores(b + 1, 1 - par, 0)
                    masked_scores(b + 1, 1 - par, 1)
                if not last_layer:
                    evacuate(b, par, 3)
                if more:
                    masked_scores(b + 1, 1 - par, 2)
                    masked_scores(b + 1, 1 - par, 3)
                split(b)
                update(b)
            over_batches(dve, body)

        @block.scalar
        def _(act):
            def front(b):
                if due(b):
                    act.wait_ge(s["hT_psum"], b)
                norm.apply(nc, act, h, x_tile(b), b, ACT.Relu).then_inc(s["h_ready"], 1)
                act.wait_ge(s["hT_psum"], b + 1)
                if due(b):
                    act.wait_ge(s["erow_psum"], b)
                nc.scalar.activation(hT[:], psT[:, 0, :, :], ACT.Copy).then_inc(s["hT_ready"], 1)

            def rises(b, par):
                act.wait_ge(s["erow_psum"], b + 1)
                if due(4 * (b - 1)):
                    act.wait_ge(s["base_ready"], 4 * (b - 1))
                nc.scalar.activation(e_row[:, par, :], psR[:], ACT.Copy, scale=SLOPE).then_inc(s["erow_ready"], 1)
                act.wait_ge(s["eown_ready"], b + 1)
                for t in range(TILES):
                    if due(4 * b + t - 3):
                        act.wait_ge(s["score_ready"], 4 * b + t - 3)
                    nc.scalar.activation(rise[:, t, :], psR[:], ACT.Relu, bias=e_own[:, par, t:t + 1],
                                         scale=1.0 - SLOPE).then_inc(s["rise_ready"], 1)

            def exponentials(b, par, t):
                act.wait_ge(s["ntop_ready"], 4 * b + t + 1)
                if due(b - 1 if last_layer else 4 * (b - 2) + t + 1):
                    act.wait_ge(s["pv_done" if last_layer else "probT_psum"], b - 1 if last_layer else 4 * (b - 2) + t + 1)
                nc.scalar.activation(prob[:, par, t, :], score[:, t, :], ACT.Exp, bias=ntop[:, t:t + 1],
                                     accum_out=total[:, par, t:t + 1]).then_inc(s["exp_ready"], 1)

            def evacuate(b, par, t):
                act.wait_ge(s["probT_psum"], 4 * b + t + 1)
                if due(b - 1):
                    act.wait_ge(s["pv_done"], b - 1)
                nc.scalar.activation(probT[:, par, :, t * P:(t + 1) * P], psT[:, t % 2, :, :], ACT.Copy
                                     ).then_inc(s["probT_act"], 1)

            def exp_negative(n):
                act.wait_ge(s["neg_ready"], n + 1)
                if due(n):
                    act.wait_ge(s["x_updated"], n)
                nc.scalar.activation(expneg[:], neg[:], ACT.Exp).then_inc(s["expneg_ready"], 1)

            front(0)
            rises(0, 0)
            for t in range(TILES):
                exponentials(0, 0, t)

            def body(i, par, more, more2):
                b = 2 * i + par
                if more:
                    front(b + 1)
                    rises(b + 1, 1 - par)
                if not last_layer:
                    evacuate(b, par, 0)
                if more:
                    exponentials(b + 1, 1 - par, 0)
                    exponentials(b + 1, 1 - par, 1)
                if not last_layer:
                    evacuate(b, par, 2)
                if more:
                    exponentials(b + 1, 1 - par, 2)
                    exponentials(b + 1, 1 - par, 3)
                exp_negative(b)
            over_batches(act, body)

        @block.tensor
        def _(pe):
            def front(b):
                pe.wait_ge(s["h_ready"], b + 1)
                if not last_layer:
                    if due(2 * (b - 1)):
                        pe.wait_ge(s["probT_act"], 2 * (b - 1))
                for t in range(TILES):
                    last = nc.tensor.transpose(psT[:, 0, t, :], h[:, t * DIM:(t + 1) * DIM], c["ident"][:])
                last.then_inc(s["hT_psum"], 1)
                pe.wait_ge(s["hT_ready"], b + 1)
                if due(b):
                    pe.wait_ge(s["wh_ready"], b)
                for t in range(TILES):
                    last = nc.tensor.matmul(psW[:, t * DIM:(t + 1) * DIM], hT[:, t * P:(t + 1) * P], w["W"][:],
                                            start=True, stop=True)
                last.then_inc(s["wh_psum"], 1)
                if due(b):
                    pe.wait_ge(s["eown_ready"], b)
                for t in range(TILES):
                    last = nc.tensor.matmul(psE[:, t:t + 1], hT[:, t * P:(t + 1) * P], w["u_own"][:],
                                            start=True, stop=True)
                last.then_inc(s["eown_psum"], 1)
                if due(4 * b):
                    pe.wait_ge(s["rise_ready"], 4 * b)
                nc.tensor.matmul(psR[:], w["u_row"][:], hT[:], start=True, stop=True).then_inc(s["erow_psum"], 1)

            def transpose_probs(b, par):
                for t in range(TILES):
                    pe.wait_ge(s["prob_ready"], 4 * b + t + 1)
                    if t == 0:
                        pe.wait_ge(s["hT_ready"], b + 1)
                    if due(2 * b + t // 2):
                        pe.wait_ge(s["probT_act" if t % 2 == 0 else "probT_dve"], 2 * b + t // 2)
                    for mt in range(TILES):
                        last = nc.tensor.transpose(psT[:, t % 2, mt, :], prob[:, par, t, mt * P:(mt + 1) * P],
                                                   c["ident"][:])
                    last.then_inc(s["probT_psum"], 1)

            def weigh(b, par):
                if due(b):
                    pe.wait_ge(s["neg_ready"], b)
                if due(b):
                    pe.wait_ge(s["pos_ready"], b)
                if last_layer:
                    pe.wait_ge(s["prob_ready"], 4 * b + 4)
                else:
                    pe.wait_ge(s["wh_ready"], b + 1)
                    pe.wait_ge(s["probT_act"], 2 * b + 2)
                    pe.wait_ge(s["probT_dve"], 2 * b + 2)
                weights, values = (prob, whs) if last_layer else (probT, wh)
                for t in range(TILES):
                    for mt in range(TILES):
                        last = nc.tensor.matmul(psO[:, t * DIM:(t + 1) * DIM], weights[:, par, mt, t * P:(t + 1) * P],
                                                values[:, par, mt * DIM:(mt + 1) * DIM],
                                                start=(mt == 0), stop=(mt == TILES - 1))
                last.then_inc(s["pv_done"], 1)

            front(0)

            def body(i, par, more, more2):
                b = 2 * i + par
                if more:
                    front(b + 1)
                if not last_layer:
                    transpose_probs(b, par)
                weigh(b, par)
            over_batches(pe, body)


def layer2(nc, c, X, adj_in, w, codes):
    KINDS = 4
    with ExitStack() as ctx:
        k = Build(nc, ctx, "kinds")
        norm = Norm(k, "norm", c)
        adj = k.sb("adj", [P, 2, TILES * NODES], BF16)
        is_kind = k.sb("is_kind", [P, KINDS - 1, TILES * NODES], U16)
        not_first = k.sb("not_first", [P, TILES * NODES], BF16)
        h = k.sb("h", [P, 2, ROW])
        hT = k.sb("hT", [P, NODES])
        haT = k.sb("haT", [P, KINDS, NODES])
        chosen = k.sb("chosen", [P, 4, NODES])
        leaky = k.sb("leaky", [P, 4, NODES])
        alpha = k.sb("alpha", [P, 2, TILES, NODES])
        xb = k.sb("xb", [P, ROW])

        psS = k.ps("psS", [P, 4, NODES])
        psA = k.ps("psA", [P, 2, TILES, 2 * P], BF16)
        psH = k.ps("psH", [P, NODES])
        psO = k.ps("psO", [P, NODES])

        adj_got = [k.sem(f"adj_got{i}") for i in range(2)]
        names = ("adjT_psum adjT_ready not_first_ready kinds_ready h_ready hT_psum hT_ready haT_ready score_psum "
                 "score_taken leaky_ready alpha_ready pv_done xb_ready x_updated")
        s = {n: k.sem(n) for n in names.split()}
        block = ctx.enter_context(nc.Block())

        def x_tile(b):
            return lambda t: X[:, bass.ds(b * ROW + t * DIM, DIM)]

        def code(b):
            return codes[:, bass.ds(b * TILES * NODES, TILES * NODES)]

        @block.gpsimd
        def _(pool):
            def load_adj(i, par):
                b = 2 * i + par
                if due(4 * (b - 1)):
                    pool.wait_ge(s["adjT_psum"], 4 * (b - 1))
                pool.dma_start(adj[:, par, :].rearrange("p (t m) -> p t m", m=NODES),
                               adj_in[bass.ds(b, 1), :, :].rearrange("b (t p) m -> p (b t) m", p=P)
                               ).then_inc(adj_got[par], 16)

            load_adj(0, 0)
            load_adj(0, 1)
            norm.on_pool(nc, pool, 0, s["h_ready"], 0)

            def body(i, par, more, more2):
                b = 2 * i + par
                if more2:
                    load_adj(i + 1, par)
                if more:
                    norm.on_pool(nc, pool, b + 1, s["h_ready"], b + 1)
                if due(b):
                    pool.wait_ge(s["x_updated"], b)
                nc.gpsimd.tensor_tensor(xb[:], X[:, bass.ds(b * ROW, ROW)], c["bias2"][:],
                                        ALU.add).then_inc(s["xb_ready"], 1)
            over_batches(pool, body)

        @block.vector
        def _(dve):
            def kinds(b):
                dve.wait_ge(s["adjT_ready"], 4 * b + 4)
                nc.vector.tensor_scalar(not_first[:], code(b), 1.0, -BIG, ALU.not_equal,
                                        ALU.mult).then_inc(s["not_first_ready"], 1)
                for kind in range(2, KINDS + 1):
                    last = nc.vector.tensor_scalar(is_kind[:, kind - 2, :], code(b), float(kind), None, ALU.is_equal)
                last.then_inc(s["kinds_ready"], 1)

            def choose(b, t):
                cols = slice(t * NODES, (t + 1) * NODES)
                u = 4 * b + t
                dve.wait_ge(s["score_psum"], 4 * u + 1)
                nc.vector.tensor_tensor(chosen[:, t, :], psS[:, 0, :], not_first[:, cols],
                                        ALU.add).then_inc(s["score_taken"], 1)
                for kind in range(2, KINDS + 1):
                    count, count_2 = held(dve, 4 * u + kind), held(dve, 4 * u + kind - 1)
                    if due(count):
                        dve.wait_ge(s["score_psum"], 1)
                        dve.wait_ge(s["score_psum"], count)
                    if due(count_2):
                        dve.wait_ge(s["score_taken"], count_2)
                    nc.vector.copy_predicated(chosen[:, t, :], is_kind[:, kind - 2, cols],
                                              psS[:, kind - 1, :]).then_inc(s["score_taken"], 1)
                if due(4 * u + KINDS):
                    dve.wait_ge(s["score_taken"], 4 * u + KINDS)
                if due(u - 3):
                    dve.wait_ge(s["alpha_ready"], u - 3)
                nc.vector.scalar_tensor_tensor(out=leaky[:, t, :], in0=chosen[:, t, :], scalar=SLOPE,
                                               in1=chosen[:, t, :], op0=ALU.mult,
                                               op1=ALU.max).then_inc(s["leaky_ready"], 1)

            def update(b):
                dve.wait_ge(s["pv_done"], b + 1)
                dve.wait_ge(s["xb_ready"], b + 1)
                nc.vector.tensor_tensor(X[:, bass.ds(b * ROW, ROW)], psO[:], xb[:], ALU.add
                                        ).then_inc(s["x_updated"], 1)

            norm.on_dve(nc, dve, x_tile(0), 0)
            kinds(0)

            def body(i, par, more, more2):
                b = 2 * i + par
                dve.wait_ge(s["not_first_ready"], b + 1)
                dve.wait_ge(s["kinds_ready"], b + 1)
                choose(b, 0)
                if more:
                    norm.on_dve(nc, dve, x_tile(b + 1), b + 1)
                for t in range(1, TILES):
                    choose(b, t)
                if more:
                    kinds(b + 1)
                update(b)
            over_batches(dve, body)

        @block.scalar
        def _(act):
            def adjacency(b):
                for t in range(TILES):
                    act.wait_ge(s["adjT_psum"], 4 * b + t + 1)
                    nc.scalar.activation(codes[:, bass.ds((b * TILES + t) * NODES, NODES)], psA[:, t % 2, :, 0:P],
                                         ACT.Copy).then_inc(s["adjT_ready"], 1)

            def hidden(b, par):
                if due(b - 1):
                    act.wait_ge(s["pv_done"], b - 1)
                norm.apply(nc, act, h[:, par, :], x_tile(b), b, ACT.Relu).then_inc(s["h_ready"], 1)

            def hidden_T(b):
                act.wait_ge(s["hT_psum"], b + 1)
                if due(16 * b):
                    act.wait_ge(s["score_psum"], 16 * b)
                nc.scalar.activation(hT[:], psH[:], ACT.Copy).then_inc(s["hT_ready"], 1)
                for kd in range(KINDS):
                    nc.scalar.activation(haT[:, kd, :], psH[:], ACT.Copy, scale=w["a"][:, kd:kd + 1]
                                         ).then_inc(s["haT_ready"], 1)

            def gates(b, par, t):
                u = 4 * b + t
                act.wait_ge(s["leaky_ready"], u + 1)
                if due(b - 1):
                    act.wait_ge(s["pv_done"], b - 1)
                nc.scalar.activation(alpha[:, par, t, :], leaky[:, t, :], ACT.Sigmoid
                                     ).then_inc(s["alpha_ready"], 1)

            adjacency(0)
            hidden(0, 0)
            hidden_T(0)

            def body(i, par, more, more2):
                b = 2 * i + par
                gates(b, par, 0)
                if more:
                    adjacency(b + 1)
                    hidden(b + 1, 1 - par)
                for t in range(1, TILES):
                    gates(b, par, t)
                if more:
                    hidden_T(b + 1)
            over_batches(act, body)

        @block.tensor
        def _(pe):
            def adjacency(i, par, b):
                pe.wait_ge(adj_got[par], 16 * (i + 1))
                for t in range(TILES):
                    if due(4 * b + t - 1):
                        pe.wait_ge(s["adjT_ready"], 4 * b + t - 1)
                    for nt in range(TILES):
                        last = nc.tensor.transpose(psA[:, t % 2, nt, 0:P],
                                                   adj[:, par, nt * NODES + t * P:nt * NODES + (t + 1) * P],
                                                   c["ident_bf"][:])
                    last.then_inc(s["adjT_psum"], 1)

            def hidden_T(b, par):
                pe.wait_ge(s["h_ready"], b + 1)
                if due(4 * b):
                    pe.wait_ge(s["haT_ready"], 4 * b)
                for t in range(TILES):
                    last = nc.tensor.transpose(psH[:, t * P:(t + 1) * P], h[:, par, t * DIM:(t + 1) * DIM],
                                               c["ident"][:])
                last.then_inc(s["hT_psum"], 1)

            def products(b, t):
                u = 4 * b + t
                if t == 0:
                    pe.wait_ge(s["hT_ready"], b + 1)
                for kd in range(KINDS):
                    if t == 0:
                        pe.wait_ge(s["haT_ready"], 4 * b + kd + 1)
                    if due(4 * (u - 1) + kd + 1):
                        pe.wait_ge(s["score_taken"], 4 * (u - 1) + kd + 1)
                    nc.tensor.matmul(psS[:, kd, :], haT[:, kd, t * P:(t + 1) * P], hT[:],
                                     start=True, stop=True).then_inc(s["score_psum"], 1)

            def weigh(b, par):
                if due(b):
                    pe.wait_ge(s["x_updated"], b)
                pe.wait_ge(s["alpha_ready"], 4 * b + 4)
                for t in range(TILES):
                    for mt in range(TILES):
                        last = nc.tensor.matmul(psO[:, t * DIM:(t + 1) * DIM], alpha[:, par, mt, t * P:(t + 1) * P],
                                                h[:, par, mt * DIM:(mt + 1) * DIM],
                                                start=(mt == 0), stop=(mt == TILES - 1))
                last.then_inc(s["pv_done"], 1)

            adjacency(0, 0, 0)
            hidden_T(0, 0)

            def body(i, par, more, more2):
                b = 2 * i + par
                products(b, 0)
                products(b, 1)
                if more:
                    adjacency(i + par, 1 - par, b + 1)
                products(b, 2)
                products(b, 3)
                if more:
                    hidden_T(b + 1, 1 - par)
                weigh(b, par)
            over_batches(pe, body)


def build(nc, t):
    with ExitStack() as ctx:
        k = Build(nc, ctx, "all")
        X = k.sb("x", [P, BATCH * ROW])
        c, w0, w1, w2, w3 = {}, {}, {}, {}, {}
        loads = []

        def const(where, name, src, shape, dt=F32):
            where[name] = k.sb(f"{src.tensor.name}_sb", shape, dt)
            loads.append((where[name], src))

        const(c, "ident", t["ident"], [P, P])
        const(c, "ident_bf", t["ident_bf"], [P, P], BF16)
        for name in ("bv", "bo", "gamma", "beta", "bias2"):
            const(c, name, t[name], [P, ROW])
        c["minus_half"], c["minus_one"] = k.sb("minus_half", [P, TILES]), k.sb("minus_one", [P, TILES])
        for name in ("wqT0", "wkT", "wvT", "woT"):
            const(w0, name, t[name], [P, DIM])
        const(w0, "bq", t["bq"], [P, 1])
        const(w0, "bk", t["bk"], [P, 1])
        const(w1, "W", t["w1"], [P, DIM])
        const(w1, "WT", t["w1T"], [P, DIM])
        const(w1, "a", t["a1"], [P, 2])
        const(w3, "W", t["w3"], [P, DIM])
        const(w3, "WT", t["w3T"], [P, DIM])
        const(w3, "a", t["a3"], [P, 2])
        const(w2, "a", t["a2"], [P, 4])
        w0["wqT"], w0["bqs"] = k.sb("wqT", [P, DIM]), k.sb("bqs", [P, 1])
        ones = k.sb("ones", [P, P])
        for name, w in (("u1", w1), ("u3", w3)):
            w["u"] = k.sb(name, [P, 2])
            w["u_row"] = k.sb(f"{name}_row", [P, P])
        w1["u_own"], w3["u_own"] = w1["u"][:, 0:1], w3["u"][:, 1:2]

        with ExitStack() as setup:
            kk = Build(nc, setup, "setup")
            psU = kk.ps("psU", [P, 4])
            got, u_psum, u_ready, ones_ready = kk.sem("got"), kk.sem("u_psum"), kk.sem("u_ready"), kk.sem("ones_ready")
            block = setup.enter_context(nc.Block())

            @block.sync
            def _(sp):
                for dst, src in loads:
                    sp.dma_start(dst[:], src).then_inc(got, 16)

            @block.tensor
            def _(pe):
                pe.wait_ge(got, 16 * len(loads))
                nc.tensor.matmul(psU[:, 0:2], w1["WT"][:], w1["a"][:], start=True, stop=True).then_inc(u_psum, 1)
                nc.tensor.matmul(psU[:, 2:4], w3["WT"][:], w3["a"][:], start=True, stop=True).then_inc(u_psum, 1)

            @block.vector
            def _(dve):
                nc.vector.memset(c["minus_half"][:], -0.5)
                nc.vector.memset(c["minus_one"][:], -1.0)
                nc.vector.memset(ones[:], 1.0).then_inc(ones_ready, 1)
                dve.wait_ge(got, 16 * len(loads))
                scale = -float(HDIM) ** -0.5
                nc.vector.tensor_scalar(w0["wqT"][:], w0["wqT0"][:], scale, None, ALU.mult)
                nc.vector.tensor_scalar(w0["bqs"][:], w0["bq"][:], scale, None, ALU.mult)
                dve.wait_ge(u_psum, 2)
                nc.vector.tensor_copy(w1["u"][:], psU[:, 0:2]).then_inc(u_ready, 1)
                nc.vector.tensor_copy(w3["u"][:], psU[:, 2:4]).then_inc(u_ready, 1)
                dve.wait_ge(u_ready, 2)
                dve.wait_ge(ones_ready, 1)
                nc.vector.tensor_scalar(w1["u_row"][:], ones[:], w1["u"][:, 1:2], None, ALU.mult)
                nc.vector.tensor_scalar(w3["u_row"][:], ones[:], w3["u"][:, 0:1], None, ALU.mult)

        layer0(nc, c, X, t["x"], t["adj"], w0)
        graph_attention(nc, c, X, t["adj"], w1, None, None, False)
        with nc.sbuf_tensor("codes", [P, BATCH * TILES * NODES], BF16) as codes:
            layer2(nc, c, X, t["adj"], w2, codes)
            graph_attention(nc, c, X, None, w3, codes, t["out"], True)


def kernel(**inputs):
    import concourse.bacc as bacc
    from concourse.bass_utils import run_bass_kernel_spmd

    f = {n: np.ascontiguousarray(a) for n, a in inputs.items()}

    def rows(v):
        return np.ascontiguousarray(np.broadcast_to(np.tile(v, TILES), (P, ROW)))

    arrays = {
        "x": f["x"], "adj": f["adj"],
        "ident": np.eye(P, dtype=np.float32), "ident_bf": np.eye(P, dtype=np.float32).astype(mybir.dt.np(BF16)),
        "wqT0": f["L0_gnn_Wq"].T, "wkT": f["L0_gnn_Wk"].T, "wvT": f["L0_gnn_Wv"].T, "woT": f["L0_gnn_Wo"].T,
        "bq": f["L0_gnn_bq"][:, None], "bk": f["L0_gnn_bk"][:, None],
        "bv": rows(f["L0_gnn_bv"]), "bo": rows(f["L0_gnn_bo"]),
        "gamma": rows(f["L0_gnn_gamma"]), "beta": rows(f["L0_gnn_beta"]), "bias2": rows(f["L2_gnn_bias"]),
        "w1": f["L1_gnn_W"], "w1T": f["L1_gnn_W"].T, "a1": f["L1_gnn_a"].reshape(2, DIM).T,
        "a2": np.concatenate([f[f"L2_gnn_a{i}"] for i in range(4)], axis=1),
        "w3": f["L3_gnn_W"], "w3T": f["L3_gnn_W"].T, "a3": f["L3_gnn_a"].reshape(2, DIM).T,
    }
    arrays = {n: np.ascontiguousarray(a) for n, a in arrays.items()}
    nc = bacc.Bacc("TRN2", target_bir_lowering=False, num_devices=1)
    t = {n: nc.dram_tensor(f"in_{n}", a.shape, mybir.dt.from_np(a.dtype), kind="ExternalInput").ap()
         for n, a in arrays.items()}
    t["out"] = nc.dram_tensor("out", (BATCH, NODES, DIM), F32, kind="ExternalOutput").ap()
    build(nc, t)
    r = run_bass_kernel_spmd(nc, [{f"in_{n}": a for n, a in arrays.items()}], core_ids=[0])
    return r.results[0]["out"]
```

```python
from contextlib import ExitStack

import numpy as np

import concourse.bass as bass
from concourse import mybir

F32 = mybir.dt.float32
F32R = mybir.dt.float32r
BF16 = mybir.dt.bfloat16
U16 = mybir.dt.uint16
ALU = mybir.AluOpType
ACT = mybir.ActivationFunctionType

P = 128
BATCH, NODES, DIM = 16, 512, 128
TILES = NODES // P
HEADS = 4
HDIM = DIM // HEADS
ROW = TILES * DIM
EPS = 1e-05
BIG = 2.0 ** 100
FAR = 3.0e38
SLOPE = 0.2


def due(count):
    return not isinstance(count, int) or count > 0


def held(eng, count):
    return count if isinstance(count, int) else eng.to_reg(count)


LAGS = 5
RAMP = 6


class Batch:

    def __init__(self, pair, par):
        self.pair, self.par, self.n = pair, par, 2 * pair + par


def stages(pair, par):
    found = []
    for lag in range(LAGS):
        d = par - lag
        i = pair + (d - d % 2) // 2
        there = not isinstance(i, int) or 0 <= 2 * i + d % 2 < BATCH
        found.append(Batch(i, d % 2) if there else None)
    return found


def over_steps(eng, step):
    for t in range(RAMP):
        step(*stages(t // 2, t % 2))
    with eng.Fori(RAMP // 2, BATCH // 2) as pair:
        for par in range(2):
            step(*stages(pair, par))
    for t in range(BATCH, BATCH + LAGS - 1):
        step(*stages(t // 2, t % 2))


class Build:

    def __init__(self, nc, ctx, layer):
        self.nc, self.ctx, self.layer = nc, ctx, layer

    def sb(self, name, shape, dt=F32):
        return self.ctx.enter_context(self.nc.sbuf_tensor(f"{self.layer}_{name}", shape, dt))

    def ps(self, name, shape, dt=F32):
        return self.ctx.enter_context(self.nc.psum_tensor(f"{self.layer}_{name}", shape, dt))

    def sem(self, name):
        return self.ctx.enter_context(self.nc.semaphore(f"{self.layer}_{name}"))


class Norm:

    def __init__(self, k, name, c):
        self.parts = k.sb(f"{name}_parts", [P, TILES, 6])
        self.mv = k.sb(f"{name}_mv", [P, TILES, 2])
        self.var = k.sb(f"{name}_var", [P, TILES])
        self.rstd = k.sb(f"{name}_rstd", [P, 2, TILES])
        self.mr = k.sb(f"{name}_mr", [P, TILES])
        self.shift = k.sb(f"{name}_shift", [P, 2, TILES])
        self.parts_done = k.sem(f"{name}_parts_done")
        self.moments = k.sem(f"{name}_moments")
        self.var_done = k.sem(f"{name}_var_done")
        self.rstd_done = k.sem(f"{name}_rstd_done")
        self.mr_done = k.sem(f"{name}_mr_done")
        self.ready = k.sem(f"{name}_ready")
        self.c = c

    def on_dve(self, nc, dve, tile, b):
        if due(b.n):
            dve.wait_ge(self.mr_done, b.n)
        for t in range(TILES):
            last = nc.vector.bn_stats(self.parts[:, t, :], tile(t))
        last.then_inc(self.parts_done, 1)
        count = held(dve, b.n + 1)
        dve.wait_ge(self.parts_done, 1)
        dve.wait_ge(self.parts_done, count)
        for t in range(TILES):
            last = nc.vector.bn_aggr(self.mv[:, t, :], self.parts[:, t, :])
        last.then_inc(self.moments, 1)

    def on_pool(self, nc, pool, b, used, used_count):
        count = held(pool, b.n + 1)
        pool.wait_ge(self.moments, 1)
        pool.wait_ge(self.moments, count)
        nc.gpsimd.tensor_scalar(self.var[:], self.mv[:, :, 1], EPS, 1.0, ALU.add, ALU.mult).then_inc(self.var_done, 1)
        pool.wait_ge(self.var_done, b.n + 1)
        if due(used_count):
            pool.wait_ge(used, used_count)
        rstd = self.rstd[:, b.par, :]
        nc.gpsimd.tensor_tensor(rstd, self.var[:], self.c["minus_half"][:], ALU.pow).then_inc(self.rstd_done, 1)
        pool.wait_ge(self.rstd_done, b.n + 1)
        nc.gpsimd.tensor_tensor(self.mr[:], self.mv[:, :, 0], rstd, ALU.mult).then_inc(self.mr_done, 1)
        count = held(pool, b.n + 1)
        pool.wait_ge(self.mr_done, 1)
        pool.wait_ge(self.mr_done, count)
        nc.gpsimd.tensor_scalar(self.shift[:, b.par, :], self.mr[:], -1.0, 1.0, ALU.mult,
                                ALU.mult).then_inc(self.ready, 1)

    def apply(self, nc, act, out, tile, b, func):
        act.wait_ge(self.ready, b.n + 1)
        for t in range(TILES):
            last = nc.scalar.activation(out[:, t * DIM:(t + 1) * DIM], tile(t), func,
                                        bias=self.shift[:, b.par, t:t + 1], scale=self.rstd[:, b.par, t:t + 1])
        return last


def x_tiles(X, b):
    return lambda t: X[:, bass.ds(b.n * ROW + t * DIM, DIM)]


def x_rows(X, b):
    return X[:, bass.ds(b.n * ROW, ROW)]


def layer0(nc, c, X, dram, w):
    PARTS = 3
    STACK = 16 * PARTS * HEADS
    with ExitStack() as ctx:
        k = Build(nc, ctx, "att")
        norm, post = Norm(k, "norm", c), Norm(k, "post", c)
        bv, bo, gamma, beta = (k.sb(name, [P, ROW]) for name in ("bv", "bo", "gamma", "beta"))
        adj = k.sb("adj", [P, 2, TILES * NODES], BF16)
        away = k.sb("away", [P, 2, TILES * NODES], BF16)
        h = k.sb("h", [P, ROW])
        hT = k.sb("hT", [P, NODES])
        qhi, qlo = k.sb("qhi", [P, NODES], F32R), k.sb("qlo", [P, NODES], F32R)
        khi, klo = k.sb("khi", [P, NODES], F32R), k.sb("klo", [P, NODES], F32R)
        qs = k.sb("qs", [PARTS * HDIM, 2, HEADS, NODES], F32R)
        ks = k.sb("ks", [PARTS * HDIM, 2, HEADS, NODES], F32R)
        V = k.sb("v", [P, 2, TILES * DIM])
        score = k.sb("score", [P, HEADS, NODES])
        low = k.sb("low", [P, HEADS])
        prob = k.sb("prob", [P, TILES, HEADS, NODES])
        total = k.sb("total", [P, TILES, HEADS])
        rtotal = k.sb("rtotal", [P, TILES, HEADS])
        probT = k.sb("probT", [P, 2, TILES, HEADS, 2 * P])
        oT = k.sb("oT", [P, NODES])
        y = k.sb("y", [P, ROW])
        yn = k.sb("yn", [P, ROW])
        yg = k.sb("yg", [P, ROW])
        yb = k.sb("yb", [P, ROW])

        psS = k.ps("psS", [P, HEADS, NODES])
        psT = k.ps("psT", [P, 2, TILES, P])
        psO = k.ps("psO", [P, NODES])
        psW = k.ps("psW", [P, NODES])

        rows_got = k.sem("rows_got")
        x_got = [k.sem(f"x_got{i}") for i in range(2)]
        adj_got = [k.sem(f"adj_got{i}") for i in range(2)]
        stacked = {n: [k.sem(f"{n}_stacked{i}") for i in range(2)] for n in "qk"}
        names = ("masked h_ready hT_psum hT_ready q_psum qhi_ready qlo_ready k_psum khi_ready klo_ready v_psum "
                 "v_ready score_psum score_ready exp_ready rtotal_ready prob_ready probT_psum probT_act probT_dve "
                 "pv_done oT_ready proj_psum y_ready yn_ready yg_ready yb_ready x_updated")
        s = {n: k.sem(n) for n in names.split()}
        block = ctx.enter_context(nc.Block())

        @block.sync
        def _(sp):
            for dst, name in ((bv, "bv"), (bo, "bo"), (gamma, "gamma"), (beta, "beta")):
                sp.dma_start(dst[:], dram[name]).then_inc(rows_got, 16)

            def step(b0, b1, b2, b3, b4):
                if b0:
                    sp.dma_start(x_rows(X, b0).rearrange("p (t c) -> p t c", c=DIM),
                                 dram["x"][bass.ds(b0.n, 1), :, :].rearrange("b (t p) c -> p (b t) c", p=P)
                                 ).then_inc(x_got[b0.par], 16)
                if not b1:
                    return
                for name, dst, hi, lo, hi_rows, lo_row in (("q", qs, qhi, qlo, (0, 1), 2), ("k", ks, khi, klo, (0, 2), 1)):
                    hi_count, lo_count, read = held(sp, b1.n + 1), held(sp, b1.n + 1), held(sp, 16 * (b1.n - 1))
                    sp.wait_ge(s[f"{name}hi_ready"], 1)
                    sp.wait_ge(s[f"{name}hi_ready"], hi_count)
                    if due(read):
                        sp.wait_ge(s["score_psum"], read)
                    for r in hi_rows:
                        for hd in range(HEADS):
                            sp.dma_start(dst[r * HDIM:(r + 1) * HDIM, b1.par, hd, :].bitcast(F32),
                                         hi[hd * HDIM:(hd + 1) * HDIM, :].bitcast(F32)
                                         ).then_inc(stacked[name][b1.par], 16)
                    sp.wait_ge(s[f"{name}lo_ready"], 1)
                    sp.wait_ge(s[f"{name}lo_ready"], lo_count)
                    for hd in range(HEADS):
                        sp.dma_start(dst[lo_row * HDIM:(lo_row + 1) * HDIM, b1.par, hd, :].bitcast(F32),
                                     lo[hd * HDIM:(hd + 1) * HDIM, :].bitcast(F32)
                                     ).then_inc(stacked[name][b1.par], 16)
            over_steps(sp, step)

        @block.gpsimd
        def _(pool):
            def divide(b, nt):
                count = held(pool, 4 * b.n + nt + 1)
                pool.wait_ge(s["rtotal_ready"], 1)
                pool.wait_ge(s["rtotal_ready"], count)
                for hd in range(HEADS):
                    pr = prob[:, nt, hd, :]
                    nc.gpsimd.tensor_scalar(pr, pr, rtotal[:, nt, hd:hd + 1], 1.0, ALU.mult,
                                            ALU.mult).then_inc(s["prob_ready"], 1)

            def step(b0, b1, b2, b3, b4):
                if b0:
                    if due(b0.n - 1):
                        pool.wait_ge(s["masked"], b0.n - 1)
                    pool.dma_start(adj[:, b0.par, :].rearrange("p (t m) -> p t m", m=NODES),
                                   dram["adj"][bass.ds(b0.n, 1), :, :].rearrange("b (t p) m -> p (b t) m", p=P)
                                   ).then_inc(adj_got[b0.par], 16)
                if b3:
                    divide(b3, 3)
                if b2:
                    divide(b2, 0)
                if b4:
                    post.on_pool(nc, pool, b4, s["yn_ready"], b4.n)
                if b2:
                    divide(b2, 1)
                if b0:
                    norm.on_pool(nc, pool, b0, s["h_ready"], b0.n)
                if b4:
                    if isinstance(b4.n, int) and b4.n == 0:
                        pool.wait_ge(rows_got, 64)
                    pool.wait_ge(s["yn_ready"], b4.n + 1)
                    nc.gpsimd.tensor_tensor(yg[:], yn[:], gamma[:], ALU.mult).then_inc(s["yg_ready"], 1)
                    pool.wait_ge(s["yg_ready"], b4.n + 1)
                    nc.gpsimd.tensor_tensor(yb[:], yg[:], beta[:], ALU.add).then_inc(s["yb_ready"], 1)
                if b2:
                    divide(b2, 2)
                if b4:
                    pool.wait_ge(s["yb_ready"], b4.n + 1)
                    nc.gpsimd.tensor_tensor(x_rows(X, b4), x_rows(X, b4), yb[:], ALU.add
                                            ).then_inc(s["x_updated"], 1)
            over_steps(pool, step)

        @block.vector
        def _(dve):
            def low_half(b, name, hi, lo, bias):
                dve.wait_ge(s[f"{name}hi_ready"], b.n + 1)
                nc.vector.scalar_tensor_tensor(out=lo[:], in0=psW[:], scalar=bias, in1=hi[:].bitcast(F32),
                                               op0=ALU.add, op1=ALU.subtract).then_inc(s[f"{name}lo_ready"], 1)

            def masked_scores(b, nt, hd):
                g = 4 * b.n + nt
                there, read = held(dve, 4 * g + hd + 1), held(dve, 4 * (g - 1) + hd + 1)
                dve.wait_ge(s["score_psum"], 1)
                dve.wait_ge(s["score_psum"], there)
                if due(read):
                    dve.wait_ge(s["exp_ready"], read)
                nc.vector.tensor_tensor_reduce(score[:, hd, :], psS[:, hd, :],
                                               away[:, b.par, nt * NODES:(nt + 1) * NODES], 1.0, FAR,
                                               ALU.add, ALU.min, low[:, hd:hd + 1]).then_inc(s["score_ready"], 1)

            def evacuate(b, nt, hd):
                dve.wait_ge(s["probT_psum"], 4 * (4 * b.n + nt) + hd + 1)
                if due(2 * b.n + nt // 2 - 1):
                    dve.wait_ge(s["pv_done"], 2 * b.n + nt // 2 - 1)
                nc.vector.tensor_copy(probT[:, nt // 2, :, hd, (nt % 2) * P:(nt % 2 + 1) * P],
                                      psT[:, hd % 2, :, :]).then_inc(s["probT_dve"], 1)

            def reciprocals(b, nt):
                dve.wait_ge(s["exp_ready"], 4 * (4 * b.n + nt) + 4)
                if due(4 * (4 * b.n + nt - TILES) + 4):
                    dve.wait_ge(s["prob_ready"], 4 * (4 * b.n + nt - TILES) + 4)
                nc.vector.reciprocal(rtotal[:, nt, :], total[:, nt, :]).then_inc(s["rtotal_ready"], 1)

            def head(b, nt, hd):
                if b:
                    masked_scores(b, nt, hd)

            def behind(before, before_nt, two_before, two_before_nt):
                if before:
                    reciprocals(before, before_nt)
                if two_before:
                    evacuate(two_before, two_before_nt, 1)

            def step(b0, b1, b2, b3, b4):
                if b4:
                    if isinstance(b4.n, int) and b4.n == 0:
                        dve.wait_ge(rows_got, 64)
                    dve.wait_ge(s["proj_psum"], b4.n + 1)
                    if due(b4.n):
                        dve.wait_ge(s["yn_ready"], b4.n)
                    nc.vector.tensor_tensor(y[:], psW[:], bo[:], ALU.add).then_inc(s["y_ready"], 1)
                if b2:
                    dve.wait_ge(s["masked"], b2.n + 1)
                head(b2, 0, 0)
                head(b2, 0, 1)
                behind(b3, 3, b3, 2)
                head(b2, 0, 2)
                head(b2, 0, 3)
                if b3:
                    evacuate(b3, 2, 3)

                head(b2, 1, 0)
                if b1:
                    low_half(b1, "q", qhi, qlo, w["bqs"][:, 0:1])
                head(b2, 1, 1)
                behind(b2, 0, b3, 3)
                head(b2, 1, 2)
                if b4:
                    dve.wait_ge(s["y_ready"], b4.n + 1)
                    post.on_dve(nc, dve, lambda t: y[:, t * DIM:(t + 1) * DIM], b4)
                head(b2, 1, 3)
                if b3:
                    evacuate(b3, 3, 3)

                head(b2, 2, 0)
                if b1:
                    low_half(b1, "k", khi, klo, w["bk"][:, 0:1])
                head(b2, 2, 1)
                behind(b2, 1, b2, 0)
                head(b2, 2, 2)
                if b0:
                    dve.wait_ge(x_got[b0.par], 16 * (b0.pair + 1))
                    norm.on_dve(nc, dve, x_tiles(X, b0), b0)
                head(b2, 2, 3)
                if b2:
                    evacuate(b2, 0, 3)

                head(b2, 3, 0)
                if b1:
                    dve.wait_ge(adj_got[b1.par], 16 * (b1.pair + 1))
                    nc.vector.tensor_scalar(away[:, b1.par, :], adj[:, b1.par, :], 0.0, BIG, ALU.is_equal,
                                            ALU.mult).then_inc(s["masked"], 1)
                head(b2, 3, 1)
                behind(b2, 2, b2, 1)
                head(b2, 3, 2)
                if b1:
                    if isinstance(b1.n, int) and b1.n == 0:
                        dve.wait_ge(rows_got, 64)
                    dve.wait_ge(s["v_psum"], b1.n + 1)
                    if due(2 * (b1.n - 1)):
                        dve.wait_ge(s["pv_done"], 2 * (b1.n - 1))
                    nc.vector.tensor_tensor(V[:, b1.par, :], psW[:], bv[:], ALU.add).then_inc(s["v_ready"], 1)
                head(b2, 3, 3)
                if b2:
                    evacuate(b2, 1, 3)
            over_steps(dve, step)

        @block.scalar
        def _(act):
            def high_half(b, name, hi, bias):
                act.wait_ge(s[f"{name}_psum"], b.n + 1)
                if due(b.n):
                    before = stages(b.pair, b.par)[1]
                    act.wait_ge(stacked[name][before.par], STACK * (before.pair + 1))
                nc.scalar.activation(hi[:], psW[:], ACT.Identity, bias=bias).then_inc(s[f"{name}hi_ready"], 1)

            def exponentials(b, nt, hd):
                g = 4 * b.n + nt
                act.wait_ge(s["score_ready"], 4 * g + hd + 1)
                if due(4 * (g - TILES) + hd + 1):
                    act.wait_ge(s["probT_psum"], 4 * (g - TILES) + hd + 1)
                nc.scalar.activation(prob[:, nt, hd, :], score[:, hd, :], ACT.Exp, bias=low[:, hd:hd + 1],
                                     scale=-1.0, accum_out=total[:, nt, hd:hd + 1]).then_inc(s["exp_ready"], 1)

            def evacuate(b, nt, hd):
                act.wait_ge(s["probT_psum"], 4 * (4 * b.n + nt) + hd + 1)
                if due(2 * b.n + nt // 2 - 1):
                    act.wait_ge(s["pv_done"], 2 * b.n + nt // 2 - 1)
                nc.scalar.activation(probT[:, nt // 2, :, hd, (nt % 2) * P:(nt % 2 + 1) * P],
                                     psT[:, hd % 2, :, :], ACT.Copy).then_inc(s["probT_act"], 1)

            def head(b, nt, hd):
                if b:
                    exponentials(b, nt, hd)

            def step(b0, b1, b2, b3, b4):
                head(b2, 0, 0)
                if b1:
                    act.wait_ge(s["hT_psum"], b1.n + 1)
                    if due(b1.n):
                        act.wait_ge(s["v_psum"], b1.n)
                    nc.scalar.activation(hT[:], psW[:], ACT.Copy).then_inc(s["hT_ready"], 1)
                if b3:
                    evacuate(b3, 2, 0)
                head(b2, 0, 1)
                head(b2, 0, 2)
                if b1:
                    high_half(b1, "q", qhi, w["bqs"][:, 0:1])
                if b3:
                    evacuate(b3, 2, 2)
                head(b2, 0, 3)

                if b3:
                    evacuate(b3, 3, 0)
                head(b2, 1, 0)
                head(b2, 1, 1)
                if b1:
                    high_half(b1, "k", khi, w["bk"][:, 0:1])
                if b3:
                    evacuate(b3, 3, 2)
                head(b2, 1, 2)
                head(b2, 1, 3)

                if b2:
                    evacuate(b2, 0, 0)
                head(b2, 2, 0)
                head(b2, 2, 1)
                if b4:
                    if due(b4.n):
                        act.wait_ge(s["yg_ready"], b4.n)
                    post.apply(nc, act, yn, lambda t: y[:, t * DIM:(t + 1) * DIM], b4,
                               ACT.Identity).then_inc(s["yn_ready"], 1)
                if b2:
                    evacuate(b2, 0, 2)
                head(b2, 2, 2)
                head(b2, 2, 3)

                if b2:
                    evacuate(b2, 1, 0)
                if b3:
                    act.wait_ge(s["pv_done"], 2 * b3.n + 2)
                    if due(b3.n):
                        act.wait_ge(s["proj_psum"], b3.n)
                    nc.scalar.activation(oT[:], psO[:], ACT.Copy).then_inc(s["oT_ready"], 1)
                head(b2, 3, 0)
                head(b2, 3, 1)
                if b2:
                    evacuate(b2, 1, 2)
                head(b2, 3, 2)
                if b0:
                    if due(b0.n):
                        act.wait_ge(s["hT_psum"], b0.n)
                    norm.apply(nc, act, h, x_tiles(X, b0), b0, ACT.Relu).then_inc(s["h_ready"], 1)
                head(b2, 3, 3)
            over_steps(act, step)

        @block.tensor
        def _(pe):
            def scores(b, nt):
                g = 4 * b.n + nt
                if nt == 0:
                    for name in "qk":
                        pe.wait_ge(stacked[name][b.par], STACK * (b.pair + 1))
                for hd in range(HEADS):
                    if due(4 * (g - 1) + hd + 1):
                        pe.wait_ge(s["score_ready"], 4 * (g - 1) + hd + 1)
                    nc.tensor.matmul(psS[:, hd, :], qs[:, b.par, hd, nt * P:(nt + 1) * P], ks[:, b.par, hd, :],
                                     start=True, stop=True).then_inc(s["score_psum"], 1)

            def transpose_probs(b, nt, heads):
                g = 4 * b.n + nt
                for hd in heads:
                    pe.wait_ge(s["prob_ready"], 4 * g + hd + 1)
                    if due(2 * g + hd // 2):
                        pe.wait_ge(s["probT_act" if hd % 2 == 0 else "probT_dve"], 2 * g + hd // 2)
                    for mt in range(TILES):
                        last = nc.tensor.transpose(psT[:, hd % 2, mt, :], prob[:, nt, hd, mt * P:(mt + 1) * P],
                                                   c["ident"][:])
                    last.then_inc(s["probT_psum"], 1)

            def weigh(b, half):
                pe.wait_ge(s["v_ready"], b.n + 1)
                pe.wait_ge(s["probT_act"], 8 * b.n + 4 * half + 4)
                pe.wait_ge(s["probT_dve"], 8 * b.n + 4 * half + 4)
                if half == 0 and due(b.n):
                    pe.wait_ge(s["oT_ready"], b.n)
                for mt in range(TILES):
                    for hd in range(HEADS):
                        last = nc.tensor.matmul(psO[hd * HDIM:(hd + 1) * HDIM, half * 2 * P:(half + 1) * 2 * P],
                                                V[:, b.par, mt * DIM + hd * HDIM:mt * DIM + (hd + 1) * HDIM],
                                                probT[:, half, mt, hd, :], start=(mt == 0), stop=(mt == TILES - 1),
                                                skip_group_check=True)
                last.then_inc(s["pv_done"], 1)

            def step(b0, b1, b2, b3, b4):
                if b2:
                    scores(b2, 0)
                if b3:
                    transpose_probs(b3, 2, (0, 1))
                if b1:
                    pe.wait_ge(s["h_ready"], b1.n + 1)
                    if b4:
                        pe.wait_ge(s["y_ready"], b4.n + 1)
                    elif due(b1.n):
                        pe.wait_ge(s["v_ready"], b1.n)
                    for t in range(TILES):
                        last = nc.tensor.transpose(psW[:, t * P:(t + 1) * P], h[:, t * DIM:(t + 1) * DIM],
                                                   c["ident"][:])
                    last.then_inc(s["hT_psum"], 1)
                if b1:
                    pe.wait_ge(s["hT_ready"], b1.n + 1)
                    nc.tensor.matmul(psW[:], w["wqT"][:], hT[:], start=True, stop=True).then_inc(s["q_psum"], 1)
                if b3:
                    transpose_probs(b3, 2, (2, 3))
                if b2:
                    scores(b2, 1)
                if b3:
                    transpose_probs(b3, 3, (0, 1))
                if b1:
                    pe.wait_ge(s["qlo_ready"], b1.n + 1)
                    nc.tensor.matmul(psW[:], w["wkT"][:], hT[:], start=True, stop=True).then_inc(s["k_psum"], 1)
                if b3:
                    weigh(b3, 0)
                    transpose_probs(b3, 3, (2, 3))
                if b2:
                    scores(b2, 2)
                    transpose_probs(b2, 0, (0, 1))
                if b1:
                    pe.wait_ge(s["klo_ready"], b1.n + 1)
                    for t in range(TILES):
                        last = nc.tensor.matmul(psW[:, t * DIM:(t + 1) * DIM], hT[:, t * P:(t + 1) * P], w["wvT"][:],
                                                start=True, stop=True)
                    last.then_inc(s["v_psum"], 1)
                if b3:
                    weigh(b3, 1)
                if b2:
                    transpose_probs(b2, 0, (2, 3))
                    scores(b2, 3)
                    transpose_probs(b2, 1, range(HEADS))
                if b3:
                    pe.wait_ge(s["oT_ready"], b3.n + 1)
                    if b1:
                        pe.wait_ge(s["v_ready"], b1.n + 1)
                    else:
                        pe.wait_ge(s["v_ready"], BATCH)
                    if due(b3.n):
                        pe.wait_ge(s["y_ready"], b3.n)
                    for t in range(TILES):
                        last = nc.tensor.matmul(psW[:, t * DIM:(t + 1) * DIM], oT[:, t * P:(t + 1) * P], w["woT"][:],
                                                start=True, stop=True)
                    last.then_inc(s["proj_psum"], 1)
            over_steps(pe, step)


def graph_attention(nc, c, X, adj_in, w, codes, out, last_layer):
    with ExitStack() as ctx:
        k = Build(nc, ctx, "gat3" if last_layer else "gat1")
        norm = Norm(k, "norm", c)
        if not last_layer:
            adj = k.sb("adj", [P, 2, TILES * NODES], BF16)
            probT = k.sb("probT", [P, TILES, NODES])
        away = k.sb("away", [P, 2, TILES * NODES], BF16)
        h = k.sb("h", [P, ROW])
        hT = k.sb("hT", [P, NODES])
        wh = k.sb("wh", [P, 2, ROW])
        whs = k.sb("whs", [P, 2, ROW])
        e_own = k.sb("e_own", [P, 2, TILES])
        e_row = k.sb("e_row", [P, 2, NODES])
        rise = k.sb("rise", [P, TILES, NODES])
        base = k.sb("base", [P, TILES, NODES])
        score = k.sb("score", [P, TILES, NODES])
        top = k.sb("top", [P, TILES])
        ntop = k.sb("ntop", [P, TILES])
        prob = k.sb("prob", [P, 2, TILES, NODES])
        total = k.sb("total", [P, 2, TILES])
        rtotal = k.sb("rtotal", [P, 2, TILES])
        neg = k.sb("neg", [P, ROW])
        pos = k.sb("pos", [P, ROW])
        expneg = k.sb("expneg", [P, ROW])

        psW = k.ps("psW", [P, NODES])
        psE = k.ps("psE", [P, NODES])
        psR = k.ps("psR", [P, 2, NODES])
        psO = k.ps("psO", [P, NODES])
        if not last_layer:
            psT = k.ps("psT", [P, 2, TILES, P])

        adj_got = [k.sem(f"adj_got{i}") for i in range(2)]
        names = ("masked h_ready hT_psum hT_ready wh_psum wh_ready eown_psum eown_ready erow_psum erow_ready "
                 "rise_ready base_ready score_ready ntop_ready exp_ready rtotal_ready prob_ready probT_psum probT_act "
                 "probT_dve pv_done neg_ready pos_ready expneg_ready x_updated")
        s = {n: k.sem(n) for n in names.split()}
        stored = [k.sem(f"stored{i}") for i in range(2)]
        block = ctx.enter_context(nc.Block())

        if last_layer:
            @block.sync
            def _(sp):
                def step(b0, b1, b2, b3, b4):
                    if b3:
                        count = held(sp, b3.n + 1)
                        sp.wait_ge(s["x_updated"], 1)
                        sp.wait_ge(s["x_updated"], count)
                        sp.dma_start(out[bass.ds(b3.n, 1), :, :].rearrange("b (t p) c -> p (b t) c", p=P),
                                     x_rows(X, b3).rearrange("p (t c) -> p t c", c=DIM)
                                     ).then_inc(stored[b3.par], 16)
                over_steps(sp, step)
                for par in range(2):
                    sp.wait_ge(stored[par], 16 * BATCH // 2)

        @block.gpsimd
        def _(pool):
            def step(b0, b1, b2, b3, b4):
                if b2:
                    pool.wait_ge(s["masked"], b2.n + 1)
                    pool.wait_ge(s["erow_ready"], b2.n + 1)
                    for t in range(TILES):
                        if due(4 * b2.n + t - 3):
                            pool.wait_ge(s["score_ready"], 4 * b2.n + t - 3)
                        nc.gpsimd.tensor_tensor(base[:, t, :], away[:, b2.par, t * NODES:(t + 1) * NODES],
                                                e_row[:, b2.par, :], ALU.add).then_inc(s["base_ready"], 1)
                if b0:
                    norm.on_pool(nc, pool, b0, s["h_ready"], b0.n - 1)
                if b0 and not last_layer:
                    if due(b0.n - 1):
                        pool.wait_ge(s["masked"], b0.n - 1)
                    pool.dma_start(adj[:, b0.par, :].rearrange("p (t m) -> p t m", m=NODES),
                                   adj_in[bass.ds(b0.n, 1), :, :].rearrange("b (t p) m -> p (b t) m", p=P)
                                   ).then_inc(adj_got[b0.par], 16)
                if b2:
                    there, used = held(pool, b2.n + 1), held(pool, b2.n - 1)
                    pool.wait_ge(s["rtotal_ready"], 1)
                    pool.wait_ge(s["rtotal_ready"], there)
                    if last_layer:
                        pool.wait_ge(s["wh_ready"], there)
                        if due(used):
                            pool.wait_ge(s["pv_done"], used)
                    for t in range(TILES):
                        if last_layer:
                            out_, in_ = (z[:, b2.par, t * DIM:(t + 1) * DIM] for z in (whs, wh))
                        else:
                            out_ = in_ = prob[:, b2.par, t, :]
                        nc.gpsimd.tensor_scalar(out_, in_, rtotal[:, b2.par, t:t + 1], 1.0, ALU.mult,
                                                ALU.mult).then_inc(s["prob_ready"], 1)
            over_steps(pool, step)

        @block.vector
        def _(dve):
            def masked_scores(b, t):
                u = 4 * b.n + t
                there, read = held(dve, u + 1), held(dve, u - 3)
                dve.wait_ge(s["rise_ready"], 1)
                dve.wait_ge(s["rise_ready"], there)
                dve.wait_ge(s["base_ready"], there)
                if due(read):
                    dve.wait_ge(s["exp_ready"], read)
                nc.vector.tensor_tensor_reduce(score[:, t, :], rise[:, t, :], base[:, t, :], 1.0, -FAR,
                                               ALU.add, ALU.max, top[:, t:t + 1]).then_inc(s["score_ready"], 1)
                dve.wait_ge(s["score_ready"], u + 1)
                nc.vector.tensor_scalar(ntop[:, t:t + 1], top[:, t:t + 1], -1.0, None,
                                        ALU.mult).then_inc(s["ntop_ready"], 1)

            def evacuate(b, t):
                dve.wait_ge(s["probT_psum"], 4 * b.n + t + 1)
                if due(b.n):
                    dve.wait_ge(s["pv_done"], b.n)
                nc.vector.tensor_copy(probT[:, :, t * P:(t + 1) * P], psT[:, t % 2, :, :]
                                      ).then_inc(s["probT_dve"], 1)

            def update(b):
                dve.wait_ge(s["expneg_ready"], b.n + 1)
                dve.wait_ge(s["pos_ready"], b.n + 1)
                nc.vector.scalar_tensor_tensor(out=x_rows(X, b), in0=expneg[:], scalar=-1.0, in1=pos[:],
                                               op0=ALU.add, op1=ALU.add).then_inc(s["x_updated"], 1)

            def copy_values(b):
                dve.wait_ge(s["wh_psum"], b.n + 1)
                if due(b.n - 1):
                    dve.wait_ge(s["pv_done"], b.n - 1)
                nc.vector.tensor_copy(wh[:, b.par, :], psW[:]).then_inc(s["wh_ready"], 1)

            def elu_parts(b):
                dve.wait_ge(s["pv_done"], b.n + 1)
                if due(b.n):
                    dve.wait_ge(s["expneg_ready"], b.n)
                nc.vector.tensor_scalar(neg[:], psO[:], 0.0, None, ALU.min).then_inc(s["neg_ready"], 1)
                if due(b.n):
                    dve.wait_ge(s["x_updated"], b.n)
                nc.vector.scalar_tensor_tensor(out=pos[:], in0=psO[:], scalar=0.0, in1=x_rows(X, b),
                                               op0=ALU.max, op1=ALU.add).then_inc(s["pos_ready"], 1)

            def step(b0, b1, b2, b3, b4):
                if b0:
                    norm.on_dve(nc, dve, x_tiles(X, b0), b0)
                if b2 and not last_layer:
                    copy_values(b2)
                if b2:
                    masked_scores(b2, 0)
                if b3 and not last_layer:
                    evacuate(b3, 1)
                if b2:
                    masked_scores(b2, 1)
                if b4 and not last_layer:
                    elu_parts(b4)
                if b2:
                    masked_scores(b2, 2)
                if b3 and not last_layer:
                    evacuate(b3, 3)
                if b2:
                    masked_scores(b2, 3)
                if b4 and not last_layer:
                    update(b4)
                if b3 and last_layer:
                    elu_parts(b3)
                if b1:
                    dve.wait_ge(s["eown_psum"], b1.n + 1)
                    if due(4 * (b1.n - 1)):
                        dve.wait_ge(s["rise_ready"], 4 * (b1.n - 1))
                    nc.vector.tensor_scalar(e_own[:, b1.par, :], psE[:, 0:TILES], 1.0 - SLOPE, None,
                                            ALU.mult).then_inc(s["eown_ready"], 1)
                if b2:
                    dve.wait_ge(s["exp_ready"], 4 * b2.n + 4)
                    nc.vector.reciprocal(rtotal[:, b2.par, :], total[:, b2.par, :]).then_inc(s["rtotal_ready"], 1)
                if b1:
                    if last_layer:
                        src = codes[:, bass.ds(b1.n * (TILES * NODES), TILES * NODES)]
                    else:
                        dve.wait_ge(adj_got[b1.par], 16 * (b1.pair + 1))
                        src = adj[:, b1.par, :]
                    if due(4 * (b1.n - 1)):
                        dve.wait_ge(s["base_ready"], 4 * (b1.n - 1))
                    nc.vector.tensor_scalar(away[:, b1.par, :], src, 0.0, -BIG, ALU.is_le,
                                            ALU.mult).then_inc(s["masked"], 1)
                if b1 and last_layer:
                    copy_values(b1)
                if b3 and last_layer:
                    update(b3)
            over_steps(dve, step)

        @block.scalar
        def _(act):
            def rises(b, t):
                if t == 0:
                    act.wait_ge(s["erow_psum"], b.n + 1)
                    act.wait_ge(s["eown_ready"], b.n + 1)
                if due(4 * b.n + t - 3):
                    act.wait_ge(s["score_ready"], 4 * b.n + t - 3)
                nc.scalar.activation(rise[:, t, :], psR[:, b.par, :], ACT.Relu, bias=e_own[:, b.par, t:t + 1],
                                     scale=1.0 - SLOPE).then_inc(s["rise_ready"], 1)

            def exponentials(b, t):
                act.wait_ge(s["ntop_ready"], 4 * b.n + t + 1)
                if last_layer:
                    if due(b.n - 1):
                        act.wait_ge(s["pv_done"], b.n - 1)
                elif due(4 * (b.n - 2) + t + 1):
                    act.wait_ge(s["probT_psum"], 4 * (b.n - 2) + t + 1)
                nc.scalar.activation(prob[:, b.par, t, :], score[:, t, :], ACT.Exp, bias=ntop[:, t:t + 1],
                                     accum_out=total[:, b.par, t:t + 1]).then_inc(s["exp_ready"], 1)

            def evacuate(b, t):
                act.wait_ge(s["probT_psum"], 4 * b.n + t + 1)
                if due(b.n):
                    act.wait_ge(s["pv_done"], b.n)
                nc.scalar.activation(probT[:, :, t * P:(t + 1) * P], psT[:, t % 2, :, :], ACT.Copy
                                     ).then_inc(s["probT_act"], 1)

            def exp_of_negatives(b):
                act.wait_ge(s["neg_ready"], b.n + 1)
                if due(b.n):
                    act.wait_ge(s["x_updated"], b.n)
                nc.scalar.activation(expneg[:], neg[:], ACT.Exp).then_inc(s["expneg_ready"], 1)

            def step(b0, b1, b2, b3, b4):
                if b2:
                    rises(b2, 0)
                if b1:
                    act.wait_ge(s["hT_psum"], b1.n + 1)
                    if due(b1.n):
                        act.wait_ge(s["wh_psum"], b1.n)
                    nc.scalar.activation(hT[:], psE[:], ACT.Copy).then_inc(s["hT_ready"], 1)
                if b2:
                    rises(b2, 1)
                if b3 and not last_layer:
                    evacuate(b3, 0)
                if b2:
                    rises(b2, 2)
                    exponentials(b2, 0)
                    rises(b2, 3)
                if b4 and not last_layer:
                    exp_of_negatives(b4)
                if b3 and not last_layer:
                    evacuate(b3, 2)
                if b2:
                    exponentials(b2, 1)
                    exponentials(b2, 2)
                    exponentials(b2, 3)
                if b3 and last_layer:
                    exp_of_negatives(b3)
                if b0:
                    if due(b0.n):
                        act.wait_ge(s["hT_psum"], b0.n)
                    norm.apply(nc, act, h, x_tiles(X, b0), b0, ACT.Relu).then_inc(s["h_ready"], 1)
                if b1:
                    act.wait_ge(s["erow_psum"], b1.n + 1)
                    if due(4 * (b1.n - 1)):
                        act.wait_ge(s["base_ready"], 4 * (b1.n - 1))
                    nc.scalar.activation(e_row[:, b1.par, :], psR[:, b1.par, :], ACT.Copy, scale=SLOPE
                                         ).then_inc(s["erow_ready"], 1)
            over_steps(act, step)

        @block.tensor
        def _(pe):
            def weigh(b):
                if due(b.n):
                    pe.wait_ge(s["neg_ready"], b.n)
                    pe.wait_ge(s["pos_ready"], b.n)
                if last_layer:
                    pe.wait_ge(s["prob_ready"], 4 * b.n + 4)
                else:
                    pe.wait_ge(s["wh_ready"], b.n + 1)
                    pe.wait_ge(s["probT_act"], 2 * b.n + 2)
                    pe.wait_ge(s["probT_dve"], 2 * b.n + 2)
                for t in range(TILES):
                    for mt in range(TILES):
                        cols = slice(t * P, (t + 1) * P)
                        weights = prob[:, b.par, mt, cols] if last_layer else probT[:, mt, cols]
                        values = (whs if last_layer else wh)[:, b.par, mt * DIM:(mt + 1) * DIM]
                        last = nc.tensor.matmul(psO[:, t * DIM:(t + 1) * DIM], weights, values,
                                                start=(mt == 0), stop=(mt == TILES - 1))
                last.then_inc(s["pv_done"], 1)

            def step(b0, b1, b2, b3, b4):
                if b1:
                    pe.wait_ge(s["h_ready"], b1.n + 1)
                    if due(b1.n):
                        pe.wait_ge(s["eown_ready"], b1.n)
                    for t in range(TILES):
                        last = nc.tensor.transpose(psE[:, t * P:(t + 1) * P], h[:, t * DIM:(t + 1) * DIM],
                                                   c["ident"][:])
                    last.then_inc(s["hT_psum"], 1)
                if b3 and not last_layer:
                    for t in range(TILES):
                        pe.wait_ge(s["prob_ready"], 4 * b3.n + t + 1)
                        if due(2 * b3.n + t // 2):
                            pe.wait_ge(s["probT_act" if t % 2 == 0 else "probT_dve"], 2 * b3.n + t // 2)
                        for mt in range(TILES):
                            last = nc.tensor.transpose(psT[:, t % 2, mt, :], prob[:, b3.par, t, mt * P:(mt + 1) * P],
                                                       c["ident"][:])
                        last.then_inc(s["probT_psum"], 1)
                if b3 and last_layer:
                    weigh(b3)
                if b1:
                    pe.wait_ge(s["hT_ready"], b1.n + 1)
                    for t in range(TILES):
                        last = nc.tensor.matmul(psE[:, t:t + 1], hT[:, t * P:(t + 1) * P], w["u_own"][:],
                                                start=True, stop=True)
                    last.then_inc(s["eown_psum"], 1)
                    if due(4 * (b1.n - 1)):
                        pe.wait_ge(s["rise_ready"], 4 * (b1.n - 1))
                        pe.wait_ge(s["erow_ready"], b1.n - 1)
                    nc.tensor.matmul(psR[:, b1.par, :], w["u_row"][:], hT[:], start=True, stop=True
                                     ).then_inc(s["erow_psum"], 1)
                    if due(b1.n):
                        pe.wait_ge(s["wh_ready"], b1.n)
                    for t in range(TILES):
                        last = nc.tensor.matmul(psW[:, t * DIM:(t + 1) * DIM], hT[:, t * P:(t + 1) * P], w["W"][:],
                                                start=True, stop=True)
                    last.then_inc(s["wh_psum"], 1)
                if b3 and not last_layer:
                    weigh(b3)
            over_steps(pe, step)


def layer2(nc, c, X, adj_in, w, codes):
    KINDS = 4
    with ExitStack() as ctx:
        k = Build(nc, ctx, "kinds")
        norm = Norm(k, "norm", c)
        adj = k.sb("adj", [P, 2, TILES * NODES], BF16)
        is_kind = k.sb("is_kind", [P, KINDS - 1, TILES * NODES], U16)
        not_first = k.sb("not_first", [P, TILES * NODES], BF16)
        h_new = k.sb("h_new", [P, ROW])
        h = k.sb("h", [P, 2, ROW])
        hT = k.sb("hT", [P, NODES])
        hhi, hlo = k.sb("hhi", [P, 2, NODES], F32R), k.sb("hlo", [P, 2, NODES], F32R)
        haT = k.sb("haT", [P, 2, NODES])
        ahi, alo = k.sb("ahi", [P, 2, KINDS, NODES], F32R), k.sb("alo", [P, 2, KINDS, NODES], F32R)
        chosen = k.sb("chosen", [P, 2, NODES])
        leaky = k.sb("leaky", [P, 2, NODES])
        alpha = k.sb("alpha", [P, 2, TILES, NODES])
        xb = k.sb("xb", [P, ROW])

        psS = k.ps("psS", [P, KINDS, NODES])
        psA = k.ps("psA", [P, 2, TILES, 2 * P], BF16)
        psH = k.ps("psH", [P, NODES])
        psO = k.ps("psO", [P, NODES])

        adj_got = [k.sem(f"adj_got{i}") for i in range(2)]
        names = ("h_new_ready adjT_psum adjT_ready not_first_ready kinds_ready h_ready hT_psum hT_ready hhi_ready hlo_ready "
                 "ahi_ready haT_ready alo_ready score_psum score_taken leaky_ready alpha_ready pv_done xb_ready "
                 "x_updated")
        s = {n: k.sem(n) for n in names.split()}
        block = ctx.enter_context(nc.Block())

        @block.gpsimd
        def _(pool):
            def step(b0, b1, b2, b3, b4):
                if b0:
                    norm.on_pool(nc, pool, b0, s["h_new_ready"], b0.n - 1)
                if b0:
                    if due(4 * (b0.n - 1)):
                        pool.wait_ge(s["adjT_psum"], 4 * (b0.n - 1))
                    pool.dma_start(adj[:, b0.par, :].rearrange("p (t m) -> p t m", m=NODES),
                                   adj_in[bass.ds(b0.n, 1), :, :].rearrange("b (t p) m -> p (b t) m", p=P)
                                   ).then_inc(adj_got[b0.par], 16)
                if b1:
                    pool.wait_ge(s["hT_ready"], b1.n + 1)
                    pool.wait_ge(s["hhi_ready"], b1.n + 1)
                    nc.gpsimd.tensor_tensor(hlo[:, b1.par, :], hT[:], hhi[:, b1.par, :].bitcast(F32),
                                            ALU.subtract).then_inc(s["hlo_ready"], 1)
                    for kd in range(KINDS):
                        u = 4 * b1.n + kd
                        read = held(pool, u - 1)
                        if due(read):
                            pool.wait_ge(s["alo_ready"], 1)
                            pool.wait_ge(s["alo_ready"], read)
                        nc.gpsimd.tensor_scalar(haT[:, kd % 2, :], hT[:], w["a"][:, kd:kd + 1], 1.0, ALU.mult,
                                                ALU.mult).then_inc(s["haT_ready"], 1)
                        pool.wait_ge(s["haT_ready"], u + 1)
                        pool.wait_ge(s["ahi_ready"], u + 1)
                        nc.gpsimd.tensor_tensor(alo[:, b1.par, kd, :], haT[:, kd % 2, :],
                                                ahi[:, b1.par, kd, :].bitcast(F32),
                                                ALU.subtract).then_inc(s["alo_ready"], 1)
                if b2:
                    if due(b2.n):
                        pool.wait_ge(s["x_updated"], b2.n)
                    nc.gpsimd.tensor_tensor(xb[:], x_rows(X, b2), c["bias2"][:], ALU.add).then_inc(s["xb_ready"], 1)
            over_steps(pool, step)

        @block.vector
        def _(dve):
            def choose(b, t):
                u = 4 * b.n + t
                halves = [slice(i * NODES // 2, (i + 1) * NODES // 2) for i in range(2)]
                cols = [slice(t * NODES + i * NODES // 2, t * NODES + (i + 1) * NODES // 2) for i in range(2)]
                dve.wait_ge(s["score_psum"], 4 * u + 1)
                if due(u - 1):
                    dve.wait_ge(s["leaky_ready"], u - 1)
                for i in range(2):
                    nc.vector.tensor_tensor(chosen[:, t % 2, halves[i]], psS[:, 0, halves[i]], not_first[:, cols[i]],
                                            ALU.add).then_inc(s["score_taken"], 1)
                for kind in range(2, KINDS + 1):
                    for i in range(2):
                        there, behind = held(dve, 4 * u + kind), held(dve, 8 * u + 2 * (kind - 2) + i + 1)
                        dve.wait_ge(s["score_psum"], 1)
                        if i == 0:
                            dve.wait_ge(s["score_psum"], there)
                        dve.wait_ge(s["score_taken"], behind)
                        nc.vector.copy_predicated(chosen[:, t % 2, halves[i]], is_kind[:, kind - 2, cols[i]],
                                                  psS[:, kind - 1, halves[i]]).then_inc(s["score_taken"], 1)
                dve.wait_ge(s["score_taken"], 8 * u + 2 * KINDS)
                if due(u - 1):
                    dve.wait_ge(s["alpha_ready"], u - 1)
                nc.vector.scalar_tensor_tensor(out=leaky[:, t % 2, :], in0=chosen[:, t % 2, :], scalar=SLOPE,
                                               in1=chosen[:, t % 2, :], op0=ALU.mult,
                                               op1=ALU.max).then_inc(s["leaky_ready"], 1)

            def step(b0, b1, b2, b3, b4):
                if b2:
                    dve.wait_ge(s["not_first_ready"], b2.n + 1)
                    dve.wait_ge(s["kinds_ready"], b2.n + 1)
                if b0:
                    norm.on_dve(nc, dve, x_tiles(X, b0), b0)
                if b2:
                    choose(b2, 0)
                if b2:
                    choose(b2, 1)
                if b3:
                    dve.wait_ge(s["pv_done"], b3.n + 1)
                    dve.wait_ge(s["xb_ready"], b3.n + 1)
                    nc.vector.tensor_tensor(x_rows(X, b3), psO[:], xb[:], ALU.add).then_inc(s["x_updated"], 1)
                if b2:
                    choose(b2, 2)
                    choose(b2, 3)
                if b1:
                    code = codes[:, bass.ds(b1.n * (TILES * NODES), TILES * NODES)]
                    dve.wait_ge(s["adjT_ready"], 4 * b1.n + 4)
                    nc.vector.tensor_scalar(not_first[:], code, 1.0, -BIG, ALU.not_equal,
                                            ALU.mult).then_inc(s["not_first_ready"], 1)
                    for kind in range(2, KINDS + 1):
                        last = nc.vector.tensor_scalar(is_kind[:, kind - 2, :], code, float(kind), None, ALU.is_equal)
                    last.then_inc(s["kinds_ready"], 1)
            over_steps(dve, step)

        @block.scalar
        def _(act):
            def gates(b, t):
                act.wait_ge(s["leaky_ready"], 4 * b.n + t + 1)
                if due(b.n - 1):
                    act.wait_ge(s["pv_done"], b.n - 1)
                nc.scalar.activation(alpha[:, b.par, t, :], leaky[:, t % 2, :], ACT.Sigmoid
                                     ).then_inc(s["alpha_ready"], 1)

            def codes_of(b, t):
                act.wait_ge(s["adjT_psum"], 4 * b.n + t + 1)
                nc.scalar.activation(codes[:, bass.ds((b.n * TILES + t) * NODES, NODES)],
                                     psA[:, t % 2, :, 0:P], ACT.Copy).then_inc(s["adjT_ready"], 1)

            def step(b0, b1, b2, b3, b4):
                if b1:
                    act.wait_ge(s["hT_psum"], b1.n + 1)
                    if due(4 * b1.n):
                        act.wait_ge(s["haT_ready"], 4 * b1.n)
                    nc.scalar.activation(hT[:], psH[:], ACT.Copy).then_inc(s["hT_ready"], 1)
                    if due(16 * (b1.n - 1)):
                        act.wait_ge(s["score_psum"], 16 * (b1.n - 1))
                    nc.scalar.activation(hhi[:, b1.par, :], psH[:], ACT.Copy).then_inc(s["hhi_ready"], 1)
                    for kd in range(KINDS):
                        nc.scalar.activation(ahi[:, b1.par, kd, :], psH[:], ACT.Copy, scale=w["a"][:, kd:kd + 1]
                                             ).then_inc(s["ahi_ready"], 1)
                if b2:
                    gates(b2, 0)
                if b1:
                    codes_of(b1, 0)
                    codes_of(b1, 1)
                if b2:
                    gates(b2, 1)
                if b1:
                    codes_of(b1, 2)
                    codes_of(b1, 3)
                    if due(b1.n - 1):
                        act.wait_ge(s["pv_done"], b1.n - 1)
                    act.wait_ge(s["h_new_ready"], b1.n + 1)
                    nc.scalar.activation(h[:, b1.par, :], h_new[:], ACT.Copy).then_inc(s["h_ready"], 1)
                if b2:
                    gates(b2, 2)
                if b0:
                    if due(b0.n):
                        act.wait_ge(s["hT_psum"], b0.n)
                        act.wait_ge(s["h_ready"], b0.n)
                    norm.apply(nc, act, h_new, x_tiles(X, b0), b0, ACT.Relu).then_inc(s["h_new_ready"], 1)
                if b2:
                    gates(b2, 3)
            over_steps(act, step)

        @block.tensor
        def _(pe):
            def products(b, t):
                u = 4 * b.n + t
                cols = slice(t * P, (t + 1) * P)
                if t == 0:
                    pe.wait_ge(s["hhi_ready"], b.n + 1)
                    pe.wait_ge(s["hlo_ready"], b.n + 1)
                for kd in range(KINDS):
                    if t == 0:
                        pe.wait_ge(s["ahi_ready"], 4 * b.n + kd + 1)
                        pe.wait_ge(s["alo_ready"], 4 * b.n + kd + 1)
                    if due(8 * (u - 1) + 2 * kd + 2):
                        pe.wait_ge(s["score_taken"], 8 * (u - 1) + 2 * kd + 2)
                    hi, lo = hhi[:, b.par, :], hlo[:, b.par, :]
                    nc.tensor.matmul(psS[:, kd, :], ahi[:, b.par, kd, cols], hi, start=True, stop=False)
                    nc.tensor.matmul(psS[:, kd, :], ahi[:, b.par, kd, cols], lo, start=False, stop=False)
                    nc.tensor.matmul(psS[:, kd, :], alo[:, b.par, kd, cols], hi, start=False, stop=True
                                     ).then_inc(s["score_psum"], 1)

            def transpose_codes(b, t):
                if t == 0:
                    pe.wait_ge(adj_got[b.par], 16 * (b.pair + 1))
                if due(4 * b.n + t - 1):
                    pe.wait_ge(s["adjT_ready"], 4 * b.n + t - 1)
                for nt in range(TILES):
                    last = nc.tensor.transpose(psA[:, t % 2, nt, 0:P],
                                               adj[:, b.par, nt * NODES + t * P:nt * NODES + (t + 1) * P],
                                               c["ident_bf"][:])
                last.then_inc(s["adjT_psum"], 1)

            def weigh(b):
                if due(b.n):
                    pe.wait_ge(s["x_updated"], b.n)
                pe.wait_ge(s["alpha_ready"], 4 * b.n + 4)
                pe.wait_ge(s["h_ready"], b.n + 1)
                for t in range(TILES):
                    for mt in range(TILES):
                        last = nc.tensor.matmul(psO[:, t * DIM:(t + 1) * DIM],
                                                alpha[:, b.par, mt, t * P:(t + 1) * P],
                                                h[:, b.par, mt * DIM:(mt + 1) * DIM],
                                                start=(mt == 0), stop=(mt == TILES - 1))
                last.then_inc(s["pv_done"], 1)

            def step(b0, b1, b2, b3, b4):
                if b1:
                    pe.wait_ge(s["h_new_ready"], b1.n + 1)
                    if due(4 * b1.n):
                        pe.wait_ge(s["ahi_ready"], 4 * b1.n)
                    for t in range(TILES):
                        last = nc.tensor.transpose(psH[:, t * P:(t + 1) * P], h_new[:, t * DIM:(t + 1) * DIM],
                                                   c["ident"][:])
                    last.then_inc(s["hT_psum"], 1)
                if b2:
                    products(b2, 0)
                if b1:
                    transpose_codes(b1, 0)
                    transpose_codes(b1, 1)
                if b3:
                    weigh(b3)
                if b2:
                    products(b2, 1)
                    products(b2, 2)
                if b1:
                    transpose_codes(b1, 2)
                    transpose_codes(b1, 3)
                if b2:
                    products(b2, 3)
            over_steps(pe, step)


def build(nc, t):
    with ExitStack() as ctx:
        k = Build(nc, ctx, "all")
        X = k.sb("x", [P, BATCH * ROW])
        c, w0, w1, w2, w3 = {}, {}, {}, {}, {}
        loads = []

        def const(where, name, src, shape, dt=F32):
            where[name] = k.sb(f"{src.tensor.name}_sb", shape, dt)
            loads.append((where[name], src))

        const(c, "ident", t["ident"], [P, P])
        const(c, "ident_bf", t["ident_bf"], [P, P], BF16)
        const(c, "bias2", t["bias2"], [P, ROW])
        c["minus_half"] = k.sb("minus_half", [P, TILES])
        for name in ("wqT0", "wkT", "wvT", "woT"):
            const(w0, name, t[name], [P, DIM])
        const(w0, "bq", t["bq"], [P, 1])
        const(w0, "bk", t["bk"], [P, 1])
        const(w1, "W", t["w1"], [P, DIM])
        const(w1, "WT", t["w1T"], [P, DIM])
        const(w1, "a", t["a1"], [P, 2])
        const(w3, "W", t["w3"], [P, DIM])
        const(w3, "WT", t["w3T"], [P, DIM])
        const(w3, "a", t["a3"], [P, 2])
        const(w2, "a", t["a2"], [P, 4])
        w0["wqT"], w0["bqs"] = k.sb("wqT", [P, DIM]), k.sb("bqs", [P, 1])
        ones = k.sb("ones", [P, P])
        for name, w in (("u1", w1), ("u3", w3)):
            w["u"] = k.sb(name, [P, 2])
            w["u_row"] = k.sb(f"{name}_row", [P, P])
        w1["u_own"], w3["u_own"] = w1["u"][:, 0:1], w3["u"][:, 1:2]

        with ExitStack() as setup:
            kk = Build(nc, setup, "setup")
            psU = kk.ps("psU", [P, 4])
            got, u_psum, u_ready, ones_ready = kk.sem("got"), kk.sem("u_psum"), kk.sem("u_ready"), kk.sem("ones_ready")
            block = setup.enter_context(nc.Block())

            @block.sync
            def _(sp):
                for dst, src in loads:
                    sp.dma_start(dst[:], src).then_inc(got, 16)

            @block.tensor
            def _(pe):
                pe.wait_ge(got, 16 * len(loads))
                nc.tensor.matmul(psU[:, 0:2], w1["WT"][:], w1["a"][:], start=True, stop=True).then_inc(u_psum, 1)
                nc.tensor.matmul(psU[:, 2:4], w3["WT"][:], w3["a"][:], start=True, stop=True).then_inc(u_psum, 1)

            @block.vector
            def _(dve):
                nc.vector.memset(c["minus_half"][:], -0.5)
                nc.vector.memset(ones[:], 1.0).then_inc(ones_ready, 1)
                dve.wait_ge(got, 16 * len(loads))
                scale = -float(HDIM) ** -0.5
                nc.vector.tensor_scalar(w0["wqT"][:], w0["wqT0"][:], scale, None, ALU.mult)
                nc.vector.tensor_scalar(w0["bqs"][:], w0["bq"][:], scale, None, ALU.mult)
                dve.wait_ge(u_psum, 2)
                nc.vector.tensor_copy(w1["u"][:], psU[:, 0:2]).then_inc(u_ready, 1)
                nc.vector.tensor_copy(w3["u"][:], psU[:, 2:4]).then_inc(u_ready, 1)
                dve.wait_ge(u_ready, 2)
                dve.wait_ge(ones_ready, 1)
                nc.vector.tensor_scalar(w1["u_row"][:], ones[:], w1["u"][:, 1:2], None, ALU.mult)
                nc.vector.tensor_scalar(w3["u_row"][:], ones[:], w3["u"][:, 0:1], None, ALU.mult)

        layer0(nc, c, X, t, w0)
        graph_attention(nc, c, X, t["adj"], w1, None, None, False)
        with nc.sbuf_tensor("codes", [P, BATCH * TILES * NODES], BF16) as codes:
            layer2(nc, c, X, t["adj"], w2, codes)
            graph_attention(nc, c, X, None, w3, codes, t["out"], True)


def kernel(**inputs):
    import concourse.bacc as bacc
    from concourse.bass_utils import run_bass_kernel_spmd

    f = {n: np.ascontiguousarray(a) for n, a in inputs.items()}

    def rows(v):
        return np.ascontiguousarray(np.broadcast_to(np.tile(v, TILES), (P, ROW)))

    arrays = {
        "x": f["x"], "adj": f["adj"],
        "ident": np.eye(P, dtype=np.float32), "ident_bf": np.eye(P, dtype=np.float32).astype(mybir.dt.np(BF16)),
        "wqT0": f["L0_gnn_Wq"].T, "wkT": f["L0_gnn_Wk"].T, "wvT": f["L0_gnn_Wv"].T, "woT": f["L0_gnn_Wo"].T,
        "bq": f["L0_gnn_bq"][:, None], "bk": f["L0_gnn_bk"][:, None],
        "bv": rows(f["L0_gnn_bv"]), "bo": rows(f["L0_gnn_bo"]),
        "gamma": rows(f["L0_gnn_gamma"]), "beta": rows(f["L0_gnn_beta"]), "bias2": rows(f["L2_gnn_bias"]),
        "w1": f["L1_gnn_W"], "w1T": f["L1_gnn_W"].T, "a1": f["L1_gnn_a"].reshape(2, DIM).T,
        "a2": np.concatenate([f[f"L2_gnn_a{i}"] for i in range(4)], axis=1),
        "w3": f["L3_gnn_W"], "w3T": f["L3_gnn_W"].T, "a3": f["L3_gnn_a"].reshape(2, DIM).T,
    }
    arrays = {n: np.ascontiguousarray(a) for n, a in arrays.items()}
    nc = bacc.Bacc("TRN2", target_bir_lowering=False, num_devices=1)
    t = {n: nc.dram_tensor(f"in_{n}", a.shape, mybir.dt.from_np(a.dtype), kind="ExternalInput").ap()
         for n, a in arrays.items()}
    t["out"] = nc.dram_tensor("out", (BATCH, NODES, DIM), F32, kind="ExternalOutput").ap()
    build(nc, t)
    r = run_bass_kernel_spmd(nc, [{f"in_{n}": a for n, a in arrays.items()}], core_ids=[0])
    return r.results[0]["out"]
```

```python
from contextlib import ExitStack

import numpy as np

import concourse.bass as bass
from concourse import mybir

F32 = mybir.dt.float32
F32R = mybir.dt.float32r
BF16 = mybir.dt.bfloat16
U16 = mybir.dt.uint16
ALU = mybir.AluOpType
ACT = mybir.ActivationFunctionType

P = 128
BATCH, NODES, DIM = 16, 512, 128
TILES = NODES // P
HEADS = 4
HDIM = DIM // HEADS
ROW = TILES * DIM
EPS = 1e-05
BIG = 2.0 ** 100
FAR = 3.0e38
SLOPE = 0.2


def due(count):
    return not isinstance(count, int) or count > 0


def held(eng, count):
    return count if isinstance(count, int) else eng.to_reg(count)


LAGS = 5
RAMP = 6


class Batch:

    def __init__(self, pair, par):
        self.pair, self.par, self.n = pair, par, 2 * pair + par


def stages(pair, par):
    found = []
    for lag in range(LAGS):
        d = par - lag
        i = pair + (d - d % 2) // 2
        there = not isinstance(i, int) or 0 <= 2 * i + d % 2 < BATCH
        found.append(Batch(i, d % 2) if there else None)
    return found


def over_steps(eng, step):
    for t in range(RAMP):
        step(*stages(t // 2, t % 2))
    with eng.Fori(RAMP // 2, BATCH // 2) as pair:
        for par in range(2):
            step(*stages(pair, par))
    for t in range(BATCH, BATCH + LAGS - 1):
        step(*stages(t // 2, t % 2))


class Build:

    def __init__(self, nc, ctx, layer):
        self.nc, self.ctx, self.layer = nc, ctx, layer

    def sb(self, name, shape, dt=F32):
        return self.ctx.enter_context(self.nc.sbuf_tensor(f"{self.layer}_{name}", shape, dt))

    def ps(self, name, shape, dt=F32):
        return self.ctx.enter_context(self.nc.psum_tensor(f"{self.layer}_{name}", shape, dt))

    def sem(self, name):
        return self.ctx.enter_context(self.nc.semaphore(f"{self.layer}_{name}"))


class Norm:

    def __init__(self, k, name, c):
        self.parts = k.sb(f"{name}_parts", [P, TILES, 6])
        self.mv = k.sb(f"{name}_mv", [P, TILES, 2])
        self.var = k.sb(f"{name}_var", [P, TILES])
        self.rstd = k.sb(f"{name}_rstd", [P, 2, TILES])
        self.mr = k.sb(f"{name}_mr", [P, TILES])
        self.shift = k.sb(f"{name}_shift", [P, 2, TILES])
        self.parts_done = k.sem(f"{name}_parts_done")
        self.moments = k.sem(f"{name}_moments")
        self.var_done = k.sem(f"{name}_var_done")
        self.rstd_done = k.sem(f"{name}_rstd_done")
        self.mr_done = k.sem(f"{name}_mr_done")
        self.ready = k.sem(f"{name}_ready")
        self.c = c

    def on_dve(self, nc, dve, tile, b):
        if due(b.n):
            dve.wait_ge(self.mr_done, b.n)
        for t in range(TILES):
            last = nc.vector.bn_stats(self.parts[:, t, :], tile(t))
        last.then_inc(self.parts_done, 1)
        count = held(dve, b.n + 1)
        dve.wait_ge(self.parts_done, 1)
        dve.wait_ge(self.parts_done, count)
        for t in range(TILES):
            last = nc.vector.bn_aggr(self.mv[:, t, :], self.parts[:, t, :])
        last.then_inc(self.moments, 1)

    def on_pool(self, nc, pool, b, used, used_count):
        count = held(pool, b.n + 1)
        pool.wait_ge(self.moments, 1)
        pool.wait_ge(self.moments, count)
        nc.gpsimd.tensor_scalar(self.var[:], self.mv[:, :, 1], EPS, 1.0, ALU.add, ALU.mult).then_inc(self.var_done, 1)
        pool.wait_ge(self.var_done, b.n + 1)
        if due(used_count):
            pool.wait_ge(used, used_count)
        rstd = self.rstd[:, b.par, :]
        nc.gpsimd.tensor_tensor(rstd, self.var[:], self.c["minus_half"][:], ALU.pow).then_inc(self.rstd_done, 1)
        pool.wait_ge(self.rstd_done, b.n + 1)
        nc.gpsimd.tensor_tensor(self.mr[:], self.mv[:, :, 0], rstd, ALU.mult).then_inc(self.mr_done, 1)
        count = held(pool, b.n + 1)
        pool.wait_ge(self.mr_done, 1)
        pool.wait_ge(self.mr_done, count)
        nc.gpsimd.tensor_scalar(self.shift[:, b.par, :], self.mr[:], -1.0, 1.0, ALU.mult,
                                ALU.mult).then_inc(self.ready, 1)

    def apply_on_dve(self, nc, dve, out, tile, b):
        dve.wait_ge(self.ready, b.n + 1)
        for t in range(TILES):
            last = nc.vector.tensor_scalar(out[:, t * DIM:(t + 1) * DIM], tile(t), self.rstd[:, b.par, t:t + 1],
                                           self.shift[:, b.par, t:t + 1], ALU.mult, ALU.add)
        return last

    def apply(self, nc, act, out, tile, b, func):
        act.wait_ge(self.ready, b.n + 1)
        for t in range(TILES):
            last = nc.scalar.activation(out[:, t * DIM:(t + 1) * DIM], tile(t), func,
                                        bias=self.shift[:, b.par, t:t + 1], scale=self.rstd[:, b.par, t:t + 1])
        return last


def x_tiles(X, b):
    return lambda t: X[:, bass.ds(b.n * ROW + t * DIM, DIM)]


def x_rows(X, b):
    return X[:, bass.ds(b.n * ROW, ROW)]


def layer0(nc, c, X, dram, w):
    PARTS = 3
    STACK = 16 * PARTS * HEADS
    with ExitStack() as ctx:
        k = Build(nc, ctx, "att")
        norm, post = Norm(k, "norm", c), Norm(k, "post", c)
        rows = k.sb("rows", [P, 4 * ROW])
        bv, bo, gamma, beta = (rows[:, i * ROW:(i + 1) * ROW] for i in range(4))
        adj = k.sb("adj", [P, 2, TILES * NODES], BF16)
        away = k.sb("away", [P, 2, TILES * NODES], BF16)
        h = k.sb("h", [P, ROW])
        hT = k.sb("hT", [P, NODES])
        qhi, qlo = k.sb("qhi", [P, NODES], F32R), k.sb("qlo", [P, NODES], F32R)
        khi, klo = k.sb("khi", [P, NODES], F32R), k.sb("klo", [P, NODES], F32R)
        qs = k.sb("qs", [PARTS * HDIM, 2, HEADS, NODES], F32R)
        ks = k.sb("ks", [PARTS * HDIM, 2, HEADS, NODES], F32R)
        V = k.sb("v", [P, 2, TILES * DIM])
        score = k.sb("score", [P, HEADS, NODES])
        low = k.sb("low", [P, HEADS])
        prob = k.sb("prob", [P, TILES, HEADS, NODES])
        total = k.sb("total", [P, TILES, HEADS])
        rtotal = k.sb("rtotal", [P, TILES, HEADS])
        probT = k.sb("probT", [P, 2, TILES, HEADS, 2 * P])
        oT = k.sb("oT", [P, NODES])
        y = k.sb("y", [P, ROW])
        yn = k.sb("yn", [P, ROW])
        yg = k.sb("yg", [P, ROW])
        yb = k.sb("yb", [P, ROW])

        psS = k.ps("psS", [P, HEADS, NODES])
        psT = k.ps("psT", [P, 2, TILES, P])
        psO = k.ps("psO", [P, NODES])
        psW = k.ps("psW", [P, NODES])

        rows_got = k.sem("rows_got")
        x_got = [k.sem(f"x_got{i}") for i in range(2)]
        adj_got = [k.sem(f"adj_got{i}") for i in range(2)]
        stacked = {n: [k.sem(f"{n}_stacked{i}") for i in range(2)] for n in "qk"}
        names = ("masked h_ready hT_psum hT_ready q_psum qhi_ready qlo_ready k_psum khi_ready klo_ready v_psum "
                 "v_ready score_psum score_ready exp_ready rtotal_ready prob_ready probT_psum probT_act probT_dve "
                 "pv_done oT_ready proj_psum y_ready yn_ready yg_ready yb_ready x_updated")
        s = {n: k.sem(n) for n in names.split()}
        block = ctx.enter_context(nc.Block())

        @block.sync
        def _(sp):
            def step(b0, b1, b2, b3, b4):
                if b0:
                    sp.dma_start(x_rows(X, b0).rearrange("p (t c) -> p t c", c=DIM),
                                 dram["x"][bass.ds(b0.n, 1), :, :].rearrange("b (t p) c -> p (b t) c", p=P)
                                 ).then_inc(x_got[b0.par], 16)
                    if isinstance(b0.n, int) and b0.n == 0:
                        sp.dma_start(rows[:], dram["rows"]).then_inc(rows_got, 16)
                if not b1:
                    return
                for name, dst, hi, lo, hi_rows, lo_row in (("q", qs, qhi, qlo, (0, 1), 2), ("k", ks, khi, klo, (0, 2), 1)):
                    hi_count, lo_count, read = held(sp, b1.n + 1), held(sp, b1.n + 1), held(sp, 16 * (b1.n - 1))
                    sp.wait_ge(s[f"{name}hi_ready"], 1)
                    sp.wait_ge(s[f"{name}hi_ready"], hi_count)
                    if due(read):
                        sp.wait_ge(s["score_psum"], read)
                    for r in hi_rows:
                        for hd in range(HEADS):
                            sp.dma_start(dst[r * HDIM:(r + 1) * HDIM, b1.par, hd, :].bitcast(F32),
                                         hi[hd * HDIM:(hd + 1) * HDIM, :].bitcast(F32)
                                         ).then_inc(stacked[name][b1.par], 16)
                    sp.wait_ge(s[f"{name}lo_ready"], 1)
                    sp.wait_ge(s[f"{name}lo_ready"], lo_count)
                    for hd in range(HEADS):
                        sp.dma_start(dst[lo_row * HDIM:(lo_row + 1) * HDIM, b1.par, hd, :].bitcast(F32),
                                     lo[hd * HDIM:(hd + 1) * HDIM, :].bitcast(F32)
                                     ).then_inc(stacked[name][b1.par], 16)
            over_steps(sp, step)

        @block.gpsimd
        def _(pool):
            def divide(b, nt):
                count = held(pool, 4 * b.n + nt + 1)
                pool.wait_ge(s["rtotal_ready"], 1)
                pool.wait_ge(s["rtotal_ready"], count)
                for hd in range(HEADS):
                    pr = prob[:, nt, hd, :]
                    nc.gpsimd.tensor_scalar(pr, pr, rtotal[:, nt, hd:hd + 1], 1.0, ALU.mult,
                                            ALU.mult).then_inc(s["prob_ready"], 1)

            def step(b0, b1, b2, b3, b4):
                if b0:
                    if due(b0.n - 1):
                        pool.wait_ge(s["masked"], b0.n - 1)
                    pool.dma_start(adj[:, b0.par, :].rearrange("p (t m) -> p t m", m=NODES),
                                   dram["adj"][bass.ds(b0.n, 1), :, :].rearrange("b (t p) m -> p (b t) m", p=P)
                                   ).then_inc(adj_got[b0.par], 16)
                if b3:
                    divide(b3, 3)
                if b2:
                    divide(b2, 0)
                if b4:
                    post.on_pool(nc, pool, b4, s["yn_ready"], b4.n)
                if b2:
                    divide(b2, 1)
                if b0:
                    norm.on_pool(nc, pool, b0, s["h_ready"], b0.n)
                if b4:
                    if isinstance(b4.n, int) and b4.n == 0:
                        pool.wait_ge(rows_got, 16)
                    pool.wait_ge(s["yn_ready"], b4.n + 1)
                    nc.gpsimd.tensor_tensor(yg[:], yn[:], gamma, ALU.mult).then_inc(s["yg_ready"], 1)
                    pool.wait_ge(s["yg_ready"], b4.n + 1)
                    nc.gpsimd.tensor_tensor(yb[:], yg[:], beta, ALU.add).then_inc(s["yb_ready"], 1)
                if b2:
                    divide(b2, 2)
                if b4:
                    pool.wait_ge(s["yb_ready"], b4.n + 1)
                    nc.gpsimd.tensor_tensor(x_rows(X, b4), x_rows(X, b4), yb[:], ALU.add
                                            ).then_inc(s["x_updated"], 1)
            over_steps(pool, step)

        @block.vector
        def _(dve):
            def low_half(b, name, hi, lo, bias):
                dve.wait_ge(s[f"{name}hi_ready"], b.n + 1)
                nc.vector.scalar_tensor_tensor(out=lo[:], in0=psW[:], scalar=bias, in1=hi[:].bitcast(F32),
                                               op0=ALU.add, op1=ALU.subtract).then_inc(s[f"{name}lo_ready"], 1)

            def masked_scores(b, nt, hd):
                g = 4 * b.n + nt
                there, read = held(dve, 4 * g + hd + 1), held(dve, 4 * (g - 1) + hd + 1)
                dve.wait_ge(s["score_psum"], 1)
                dve.wait_ge(s["score_psum"], there)
                if due(read):
                    dve.wait_ge(s["exp_ready"], read)
                nc.vector.tensor_tensor_reduce(score[:, hd, :], psS[:, hd, :],
                                               away[:, b.par, nt * NODES:(nt + 1) * NODES], 1.0, FAR,
                                               ALU.add, ALU.min, low[:, hd:hd + 1]).then_inc(s["score_ready"], 1)

            def evacuate(b, nt, hd):
                dve.wait_ge(s["probT_psum"], 4 * (4 * b.n + nt) + hd + 1)
                if due(2 * b.n + nt // 2 - 1):
                    dve.wait_ge(s["pv_done"], 2 * b.n + nt // 2 - 1)
                nc.vector.tensor_copy(probT[:, nt // 2, :, hd, (nt % 2) * P:(nt % 2 + 1) * P],
                                      psT[:, hd % 2, :, :]).then_inc(s["probT_dve"], 1)

            def reciprocals(b, nt):
                dve.wait_ge(s["exp_ready"], 4 * (4 * b.n + nt) + 4)
                if due(4 * (4 * b.n + nt - TILES) + 4):
                    dve.wait_ge(s["prob_ready"], 4 * (4 * b.n + nt - TILES) + 4)
                nc.vector.reciprocal(rtotal[:, nt, :], total[:, nt, :]).then_inc(s["rtotal_ready"], 1)

            def head(b, nt, hd):
                if b:
                    masked_scores(b, nt, hd)

            def behind(before, before_nt, two_before, two_before_nt):
                if before:
                    reciprocals(before, before_nt)
                if two_before:
                    evacuate(two_before, two_before_nt, 1)

            def step(b0, b1, b2, b3, b4):
                if b2:
                    dve.wait_ge(s["masked"], b2.n + 1)
                head(b2, 0, 0)
                head(b2, 0, 1)
                behind(b3, 3, b3, 2)
                head(b2, 0, 2)
                head(b2, 0, 3)

                head(b2, 1, 0)
                if b1:
                    low_half(b1, "q", qhi, qlo, w["bqs"][:, 0:1])
                head(b2, 1, 1)
                behind(b2, 0, b3, 3)
                head(b2, 1, 2)
                if b4:
                    dve.wait_ge(s["y_ready"], b4.n + 1)
                    post.on_dve(nc, dve, lambda t: y[:, t * DIM:(t + 1) * DIM], b4)
                head(b2, 1, 3)

                head(b2, 2, 0)
                if b1:
                    low_half(b1, "k", khi, klo, w["bk"][:, 0:1])
                head(b2, 2, 1)
                behind(b2, 1, b2, 0)
                head(b2, 2, 2)
                if b0:
                    dve.wait_ge(x_got[b0.par], 16 * (b0.pair + 1))
                    norm.on_dve(nc, dve, x_tiles(X, b0), b0)
                head(b2, 2, 3)
                if b4:
                    if due(b4.n):
                        dve.wait_ge(s["yg_ready"], b4.n)
                    post.apply_on_dve(nc, dve, yn, lambda t: y[:, t * DIM:(t + 1) * DIM], b4
                                      ).then_inc(s["yn_ready"], 1)

                head(b2, 3, 0)
                head(b2, 3, 1)
                behind(b2, 2, b2, 1)
                if b1:
                    if isinstance(b1.n, int) and b1.n == 0:
                        dve.wait_ge(rows_got, 16)
                    dve.wait_ge(s["v_psum"], b1.n + 1)
                    if due(2 * (b1.n - 1)):
                        dve.wait_ge(s["pv_done"], 2 * (b1.n - 1))
                    nc.vector.tensor_tensor(V[:, b1.par, :], psW[:], bv, ALU.add).then_inc(s["v_ready"], 1)
                if b0:
                    if due(b0.n):
                        dve.wait_ge(s["hT_psum"], b0.n)
                    norm.apply_on_dve(nc, dve, h, x_tiles(X, b0), b0).then_inc(s["h_ready"], 1)
                head(b2, 3, 2)
                if b1:
                    dve.wait_ge(adj_got[b1.par], 16 * (b1.pair + 1))
                    nc.vector.tensor_scalar(away[:, b1.par, :], adj[:, b1.par, :], 0.0, BIG, ALU.is_equal,
                                            ALU.mult).then_inc(s["masked"], 1)
                if b3:
                    if isinstance(b3.n, int) and b3.n == 0:
                        dve.wait_ge(rows_got, 16)
                    dve.wait_ge(s["proj_psum"], b3.n + 1)
                    if due(b3.n):
                        dve.wait_ge(s["yn_ready"], b3.n)
                    nc.vector.tensor_tensor(y[:], psW[:], bo, ALU.add).then_inc(s["y_ready"], 1)
                head(b2, 3, 3)
            over_steps(dve, step)

        @block.scalar
        def _(act):
            def high_half(b, name, hi, bias):
                act.wait_ge(s[f"{name}_psum"], b.n + 1)
                if due(b.n):
                    before = stages(b.pair, b.par)[1]
                    act.wait_ge(stacked[name][before.par], STACK * (before.pair + 1))
                nc.scalar.activation(hi[:], psW[:], ACT.Identity, bias=bias).then_inc(s[f"{name}hi_ready"], 1)

            def exponentials(b, nt, hd):
                g = 4 * b.n + nt
                act.wait_ge(s["score_ready"], 4 * g + hd + 1)
                if due(4 * (g - TILES) + hd + 1):
                    act.wait_ge(s["probT_psum"], 4 * (g - TILES) + hd + 1)
                nc.scalar.activation(prob[:, nt, hd, :], score[:, hd, :], ACT.Exp, bias=low[:, hd:hd + 1],
                                     scale=-1.0, accum_out=total[:, nt, hd:hd + 1]).then_inc(s["exp_ready"], 1)

            def evacuate(b, nt, hd):
                act.wait_ge(s["probT_psum"], 4 * (4 * b.n + nt) + hd + 1)
                if due(2 * b.n + nt // 2 - 1):
                    act.wait_ge(s["pv_done"], 2 * b.n + nt // 2 - 1)
                nc.scalar.activation(probT[:, nt // 2, :, hd, (nt % 2) * P:(nt % 2 + 1) * P],
                                     psT[:, hd % 2, :, :], ACT.Copy).then_inc(s["probT_act"], 1)

            def head(b, nt, hd):
                if b:
                    exponentials(b, nt, hd)

            def step(b0, b1, b2, b3, b4):
                if b1:
                    act.wait_ge(s["hT_psum"], b1.n + 1)
                    if due(b1.n):
                        act.wait_ge(s["v_psum"], b1.n)
                    nc.scalar.activation(hT[:], psW[:], ACT.Relu).then_inc(s["hT_ready"], 1)
                head(b2, 0, 0)
                if b3:
                    evacuate(b3, 2, 0)
                head(b2, 0, 1)
                if b1:
                    high_half(b1, "q", qhi, w["bqs"][:, 0:1])
                head(b2, 0, 2)
                if b3:
                    evacuate(b3, 2, 2)
                head(b2, 0, 3)
                if b3:
                    evacuate(b3, 2, 3)

                if b3:
                    evacuate(b3, 3, 0)
                head(b2, 1, 0)
                head(b2, 1, 1)
                if b1:
                    high_half(b1, "k", khi, w["bk"][:, 0:1])
                if b3:
                    evacuate(b3, 3, 2)
                head(b2, 1, 2)
                if b3:
                    evacuate(b3, 3, 3)
                head(b2, 1, 3)

                head(b2, 2, 0)
                if b2:
                    evacuate(b2, 0, 0)
                head(b2, 2, 1)
                if b2:
                    evacuate(b2, 0, 2)
                head(b2, 2, 2)
                if b2:
                    evacuate(b2, 0, 3)
                head(b2, 2, 3)

                if b2:
                    evacuate(b2, 1, 0)
                head(b2, 3, 0)
                if b3:
                    act.wait_ge(s["pv_done"], 2 * b3.n + 2)
                    if due(b3.n):
                        act.wait_ge(s["proj_psum"], b3.n)
                    nc.scalar.activation(oT[:], psO[:], ACT.Copy).then_inc(s["oT_ready"], 1)
                head(b2, 3, 1)
                if b2:
                    evacuate(b2, 1, 2)
                head(b2, 3, 2)
                if b2:
                    evacuate(b2, 1, 3)
                head(b2, 3, 3)
            over_steps(act, step)

        @block.tensor
        def _(pe):
            def scores(b, nt, heads=range(HEADS)):
                g = 4 * b.n + nt
                if nt == 0:
                    for name in "qk":
                        pe.wait_ge(stacked[name][b.par], STACK * (b.pair + 1))
                for hd in heads:
                    if due(4 * (g - 1) + hd + 1):
                        pe.wait_ge(s["score_ready"], 4 * (g - 1) + hd + 1)
                    nc.tensor.matmul(psS[:, hd, :], qs[:, b.par, hd, nt * P:(nt + 1) * P], ks[:, b.par, hd, :],
                                     start=True, stop=True).then_inc(s["score_psum"], 1)

            def transpose_probs(b, nt, heads):
                g = 4 * b.n + nt
                for hd in heads:
                    pe.wait_ge(s["prob_ready"], 4 * g + hd + 1)
                    if hd == 3:
                        pe.wait_ge(s["probT_dve"], g + 1)
                    elif due(3 * g + hd - 1):
                        pe.wait_ge(s["probT_act"], 3 * g + hd - 1)
                    for mt in range(TILES):
                        last = nc.tensor.transpose(psT[:, hd % 2, mt, :], prob[:, nt, hd, mt * P:(mt + 1) * P],
                                                   c["ident"])
                    last.then_inc(s["probT_psum"], 1)

            def weigh(b, half, tiles):
                if tiles[0] == 0:
                    pe.wait_ge(s["v_ready"], b.n + 1)
                    pe.wait_ge(s["probT_act"], 3 * (4 * b.n + 2 * half + 2))
                    pe.wait_ge(s["probT_dve"], 4 * b.n + 2 * half + 2)
                    if half == 0 and due(b.n):
                        pe.wait_ge(s["oT_ready"], b.n)
                for mt in tiles:
                    for hd in range(HEADS):
                        last = nc.tensor.matmul(psO[hd * HDIM:(hd + 1) * HDIM, half * 2 * P:(half + 1) * 2 * P],
                                                V[:, b.par, mt * DIM + hd * HDIM:mt * DIM + (hd + 1) * HDIM],
                                                probT[:, half, mt, hd, :], start=(mt == 0), stop=(mt == TILES - 1),
                                                skip_group_check=True)
                if tiles[-1] == TILES - 1:
                    last.then_inc(s["pv_done"], 1)

            def step(b0, b1, b2, b3, b4):
                if b1:
                    pe.wait_ge(s["h_ready"], b1.n + 1)
                    if b4:
                        pe.wait_ge(s["y_ready"], b4.n + 1)
                    elif due(b1.n):
                        pe.wait_ge(s["v_ready"], b1.n)
                    for t in range(TILES):
                        last = nc.tensor.transpose(psW[:, t * P:(t + 1) * P], h[:, t * DIM:(t + 1) * DIM],
                                                   c["ident"])
                    last.then_inc(s["hT_psum"], 1)
                if b2:
                    scores(b2, 0, (0, 1))
                if b3:
                    transpose_probs(b3, 2, (0, 1))
                if b1:
                    pe.wait_ge(s["hT_ready"], b1.n + 1)
                    nc.tensor.matmul(psW[:], w["wqT"][:], hT[:], start=True, stop=True).then_inc(s["q_psum"], 1)
                if b2:
                    scores(b2, 0, (2, 3))
                if b3:
                    transpose_probs(b3, 2, (2, 3))
                if b2:
                    scores(b2, 1)
                if b3:
                    transpose_probs(b3, 3, (0, 1))
                if b1:
                    pe.wait_ge(s["qlo_ready"], b1.n + 1)
                    nc.tensor.matmul(psW[:], w["wkT"], hT[:], start=True, stop=True).then_inc(s["k_psum"], 1)
                if b3:
                    transpose_probs(b3, 3, (2, 3))
                    weigh(b3, 0, (0, 1))
                if b2:
                    scores(b2, 2)
                    transpose_probs(b2, 0, (0, 1))
                if b3:
                    weigh(b3, 0, (2, 3))
                if b1:
                    pe.wait_ge(s["klo_ready"], b1.n + 1)
                    for t in range(TILES):
                        last = nc.tensor.matmul(psW[:, t * DIM:(t + 1) * DIM], hT[:, t * P:(t + 1) * P], w["wvT"],
                                                start=True, stop=True)
                    last.then_inc(s["v_psum"], 1)
                if b2:
                    transpose_probs(b2, 0, (2, 3))
                if b3:
                    weigh(b3, 1, (0, 1))
                if b2:
                    scores(b2, 3)
                    transpose_probs(b2, 1, (0, 1))
                if b3:
                    weigh(b3, 1, (2, 3))
                if b2:
                    transpose_probs(b2, 1, (2, 3))
                if b3:
                    pe.wait_ge(s["oT_ready"], b3.n + 1)
                    if b1:
                        pe.wait_ge(s["v_ready"], b1.n + 1)
                    else:
                        pe.wait_ge(s["v_ready"], BATCH)
                    if due(b3.n):
                        pe.wait_ge(s["y_ready"], b3.n)
                    for t in range(TILES):
                        last = nc.tensor.matmul(psW[:, t * DIM:(t + 1) * DIM], oT[:, t * P:(t + 1) * P], w["woT"],
                                                start=True, stop=True)
                    last.then_inc(s["proj_psum"], 1)
            over_steps(pe, step)


def graph_attention(nc, c, X, adj_in, w, codes, out, last_layer):
    with ExitStack() as ctx:
        k = Build(nc, ctx, "gat3" if last_layer else "gat1")
        norm = Norm(k, "norm", c)
        if not last_layer:
            adj = k.sb("adj", [P, 2, TILES * NODES], BF16)
            probT = k.sb("probT", [P, TILES, NODES])
        away = k.sb("away", [P, 2, TILES * NODES], BF16)
        h = k.sb("h", [P, ROW])
        hT = k.sb("hT", [P, NODES])
        wh = k.sb("wh", [P, 2, ROW])
        whs = k.sb("whs", [P, 2, ROW])
        e_own = k.sb("e_own", [P, 2, TILES])
        e_row = k.sb("e_row", [P, 2, NODES])
        rise = k.sb("rise", [P, TILES, NODES])
        base = k.sb("base", [P, TILES, NODES])
        score = k.sb("score", [P, TILES, NODES])
        top = k.sb("top", [P, TILES])
        ntop = k.sb("ntop", [P, TILES])
        prob = k.sb("prob", [P, 2, TILES, NODES])
        total = k.sb("total", [P, 2, TILES])
        rtotal = k.sb("rtotal", [P, 2, TILES])
        neg = k.sb("neg", [P, ROW])
        pos = k.sb("pos", [P, ROW])
        expneg = k.sb("expneg", [P, ROW])

        psW = k.ps("psW", [P, NODES])
        psE = k.ps("psE", [P, NODES])
        psR = k.ps("psR", [P, 2, NODES])
        psO = k.ps("psO", [P, NODES])
        if not last_layer:
            psT = k.ps("psT", [P, 2, TILES, P])

        adj_got = [k.sem(f"adj_got{i}") for i in range(2)]
        names = ("masked h_ready hT_psum hT_ready wh_psum wh_ready eown_psum eown_ready erow_psum erow_ready "
                 "rise_ready base_ready score_ready ntop_ready exp_ready rtotal_ready prob_ready prob_dve probT_psum probT_act "
                 "probT_dve pv_done neg_ready pos_ready expneg_ready x_updated")
        s = {n: k.sem(n) for n in names.split()}
        stored = [k.sem(f"stored{i}") for i in range(2)]
        block = ctx.enter_context(nc.Block())

        if last_layer:
            @block.sync
            def _(sp):
                def step(b0, b1, b2, b3, b4):
                    if b3:
                        count = held(sp, b3.n + 1)
                        sp.wait_ge(s["x_updated"], 1)
                        sp.wait_ge(s["x_updated"], count)
                        sp.dma_start(out[bass.ds(b3.n, 1), :, :].rearrange("b (t p) c -> p (b t) c", p=P),
                                     x_rows(X, b3).rearrange("p (t c) -> p t c", c=DIM)
                                     ).then_inc(stored[b3.par], 16)
                over_steps(sp, step)
                for par in range(2):
                    sp.wait_ge(stored[par], 16 * BATCH // 2)

        @block.gpsimd
        def _(pool):
            def step(b0, b1, b2, b3, b4):
                if b2:
                    pool.wait_ge(s["masked"], b2.n + 1)
                    pool.wait_ge(s["erow_ready"], b2.n + 1)
                    for t in range(TILES):
                        if due(4 * b2.n + t - 3):
                            pool.wait_ge(s["score_ready"], 4 * b2.n + t - 3)
                        nc.gpsimd.tensor_tensor(base[:, t, :], away[:, b2.par, t * NODES:(t + 1) * NODES],
                                                e_row[:, b2.par, :], ALU.add).then_inc(s["base_ready"], 1)
                if b0:
                    norm.on_pool(nc, pool, b0, s["h_ready"], b0.n - 1)
                if b0 and not last_layer:
                    if due(b0.n - 1):
                        pool.wait_ge(s["masked"], b0.n - 1)
                    pool.dma_start(adj[:, b0.par, :].rearrange("p (t m) -> p t m", m=NODES),
                                   adj_in[bass.ds(b0.n, 1), :, :].rearrange("b (t p) m -> p (b t) m", p=P)
                                   ).then_inc(adj_got[b0.par], 16)
                if b2:
                    there, used = held(pool, b2.n + 1), held(pool, b2.n - 1)
                    pool.wait_ge(s["rtotal_ready"], 1)
                    pool.wait_ge(s["rtotal_ready"], there)
                    if last_layer:
                        pool.wait_ge(s["wh_ready"], there)
                        if due(used):
                            pool.wait_ge(s["pv_done"], used)
                    for t in range(0 if last_layer else TILES // 2, TILES):
                        if last_layer:
                            out_, in_ = (z[:, b2.par, t * DIM:(t + 1) * DIM] for z in (whs, wh))
                        else:
                            out_ = in_ = prob[:, b2.par, t, :]
                        nc.gpsimd.tensor_scalar(out_, in_, rtotal[:, b2.par, t:t + 1], 1.0, ALU.mult,
                                                ALU.mult).then_inc(s["prob_ready"], 1)
            over_steps(pool, step)

        @block.vector
        def _(dve):
            def masked_scores(b, t):
                u = 4 * b.n + t
                there, read = held(dve, u + 1), held(dve, u - 3)
                dve.wait_ge(s["rise_ready"], 1)
                dve.wait_ge(s["rise_ready"], there)
                dve.wait_ge(s["base_ready"], there)
                if due(read):
                    dve.wait_ge(s["exp_ready"], read)
                nc.vector.tensor_tensor_reduce(score[:, t, :], rise[:, t, :], base[:, t, :], 1.0, -FAR,
                                               ALU.add, ALU.max, top[:, t:t + 1]).then_inc(s["score_ready"], 1)
                dve.wait_ge(s["score_ready"], u + 1)
                nc.vector.tensor_scalar(ntop[:, t:t + 1], top[:, t:t + 1], -1.0, None,
                                        ALU.mult).then_inc(s["ntop_ready"], 1)

            def evacuate(b, t):
                dve.wait_ge(s["probT_psum"], 4 * b.n + t + 1)
                if due(b.n):
                    dve.wait_ge(s["pv_done"], b.n)
                nc.vector.tensor_copy(probT[:, :, t * P:(t + 1) * P], psT[:, t % 2, :, :]
                                      ).then_inc(s["probT_dve"], 1)

            def update(b):
                dve.wait_ge(s["expneg_ready"], b.n + 1)
                dve.wait_ge(s["pos_ready"], b.n + 1)
                nc.vector.scalar_tensor_tensor(out=x_rows(X, b), in0=expneg[:], scalar=-1.0, in1=pos[:],
                                               op0=ALU.add, op1=ALU.add).then_inc(s["x_updated"], 1)

            def copy_values(b):
                dve.wait_ge(s["wh_psum"], b.n + 1)
                if due(b.n - 1):
                    dve.wait_ge(s["pv_done"], b.n - 1)
                nc.vector.tensor_copy(wh[:, b.par, :], psW[:]).then_inc(s["wh_ready"], 1)

            def elu_parts(b):
                dve.wait_ge(s["pv_done"], b.n + 1)
                if due(b.n):
                    dve.wait_ge(s["expneg_ready"], b.n)
                nc.vector.tensor_scalar(neg[:], psO[:], 0.0, None, ALU.min).then_inc(s["neg_ready"], 1)
                if due(b.n):
                    dve.wait_ge(s["x_updated"], b.n)
                nc.vector.scalar_tensor_tensor(out=pos[:], in0=psO[:], scalar=0.0, in1=x_rows(X, b),
                                               op0=ALU.max, op1=ALU.add).then_inc(s["pos_ready"], 1)

            def step(b0, b1, b2, b3, b4):
                if b0:
                    norm.on_dve(nc, dve, x_tiles(X, b0), b0)
                if b2 and not last_layer:
                    copy_values(b2)
                if b2:
                    masked_scores(b2, 0)
                if b3 and not last_layer:
                    evacuate(b3, 1)
                if b2:
                    masked_scores(b2, 1)
                if b4 and not last_layer:
                    elu_parts(b4)
                if b2:
                    masked_scores(b2, 2)
                if b3 and not last_layer:
                    evacuate(b3, 3)
                if b2:
                    masked_scores(b2, 3)
                if b4 and not last_layer:
                    update(b4)
                if b3 and last_layer:
                    elu_parts(b3)
                if b1:
                    dve.wait_ge(s["eown_psum"], b1.n + 1)
                    if due(4 * (b1.n - 1)):
                        dve.wait_ge(s["rise_ready"], 4 * (b1.n - 1))
                    nc.vector.tensor_scalar(e_own[:, b1.par, :], psE[:, 0:TILES], 1.0 - SLOPE, None,
                                            ALU.mult).then_inc(s["eown_ready"], 1)
                if b2:
                    dve.wait_ge(s["exp_ready"], 4 * b2.n + 4)
                    nc.vector.reciprocal(rtotal[:, b2.par, :], total[:, b2.par, :]).then_inc(s["rtotal_ready"], 1)
                if b2 and not last_layer:
                    dve.wait_ge(s["rtotal_ready"], b2.n + 1)
                    for t in range(TILES // 2):
                        pr = prob[:, b2.par, t, :]
                        nc.vector.tensor_scalar(pr, pr, rtotal[:, b2.par, t:t + 1], None,
                                                ALU.mult).then_inc(s["prob_dve"], 1)
                if b1:
                    if last_layer:
                        src = codes[:, bass.ds(b1.n * (TILES * NODES), TILES * NODES)]
                    else:
                        dve.wait_ge(adj_got[b1.par], 16 * (b1.pair + 1))
                        src = adj[:, b1.par, :]
                    if due(4 * (b1.n - 1)):
                        dve.wait_ge(s["base_ready"], 4 * (b1.n - 1))
                    nc.vector.tensor_scalar(away[:, b1.par, :], src, 0.0, -BIG, ALU.is_le,
                                            ALU.mult).then_inc(s["masked"], 1)
                if b1 and last_layer:
                    copy_values(b1)
                if b3 and last_layer:
                    update(b3)
            over_steps(dve, step)

        @block.scalar
        def _(act):
            def rises(b, t):
                if t == 0:
                    act.wait_ge(s["erow_psum"], b.n + 1)
                    act.wait_ge(s["eown_ready"], b.n + 1)
                if due(4 * b.n + t - 3):
                    act.wait_ge(s["score_ready"], 4 * b.n + t - 3)
                nc.scalar.activation(rise[:, t, :], psR[:, b.par, :], ACT.Relu, bias=e_own[:, b.par, t:t + 1],
                                     scale=1.0 - SLOPE).then_inc(s["rise_ready"], 1)

            def exponentials(b, t):
                act.wait_ge(s["ntop_ready"], 4 * b.n + t + 1)
                if last_layer:
                    if due(b.n - 1):
                        act.wait_ge(s["pv_done"], b.n - 1)
                elif due(4 * (b.n - 2) + t + 1):
                    act.wait_ge(s["probT_psum"], 4 * (b.n - 2) + t + 1)
                nc.scalar.activation(prob[:, b.par, t, :], score[:, t, :], ACT.Exp, bias=ntop[:, t:t + 1],
                                     accum_out=total[:, b.par, t:t + 1]).then_inc(s["exp_ready"], 1)

            def evacuate(b, t):
                act.wait_ge(s["probT_psum"], 4 * b.n + t + 1)
                if due(b.n):
                    act.wait_ge(s["pv_done"], b.n)
                nc.scalar.activation(probT[:, :, t * P:(t + 1) * P], psT[:, t % 2, :, :], ACT.Copy
                                     ).then_inc(s["probT_act"], 1)

            def exp_of_negatives(b):
                act.wait_ge(s["neg_ready"], b.n + 1)
                if due(b.n):
                    act.wait_ge(s["x_updated"], b.n)
                nc.scalar.activation(expneg[:], neg[:], ACT.Exp).then_inc(s["expneg_ready"], 1)

            def step(b0, b1, b2, b3, b4):
                if b2:
                    rises(b2, 0)
                if b1:
                    act.wait_ge(s["hT_psum"], b1.n + 1)
                    if due(b1.n):
                        act.wait_ge(s["wh_psum"], b1.n)
                    nc.scalar.activation(hT[:], psE[:], ACT.Copy).then_inc(s["hT_ready"], 1)
                if b2:
                    rises(b2, 1)
                if b3 and not last_layer:
                    evacuate(b3, 0)
                if b2:
                    rises(b2, 2)
                    exponentials(b2, 0)
                    rises(b2, 3)
                if b4 and not last_layer:
                    exp_of_negatives(b4)
                if b3 and not last_layer:
                    evacuate(b3, 2)
                if b2:
                    exponentials(b2, 1)
                    exponentials(b2, 2)
                    exponentials(b2, 3)
                if b3 and last_layer:
                    exp_of_negatives(b3)
                if b0:
                    if due(b0.n):
                        act.wait_ge(s["hT_psum"], b0.n)
                    norm.apply(nc, act, h, x_tiles(X, b0), b0, ACT.Relu).then_inc(s["h_ready"], 1)
                if b1:
                    act.wait_ge(s["erow_psum"], b1.n + 1)
                    if due(4 * (b1.n - 1)):
                        act.wait_ge(s["base_ready"], 4 * (b1.n - 1))
                    nc.scalar.activation(e_row[:, b1.par, :], psR[:, b1.par, :], ACT.Copy, scale=SLOPE
                                         ).then_inc(s["erow_ready"], 1)
            over_steps(act, step)

        @block.tensor
        def _(pe):
            def weigh(b):
                if due(b.n):
                    pe.wait_ge(s["neg_ready"], b.n)
                    pe.wait_ge(s["pos_ready"], b.n)
                if last_layer:
                    pe.wait_ge(s["prob_ready"], 4 * b.n + 4)
                else:
                    pe.wait_ge(s["wh_ready"], b.n + 1)
                    pe.wait_ge(s["probT_act"], 2 * b.n + 2)
                    pe.wait_ge(s["probT_dve"], 2 * b.n + 2)
                for t in range(TILES):
                    for mt in range(TILES):
                        cols = slice(t * P, (t + 1) * P)
                        weights = prob[:, b.par, mt, cols] if last_layer else probT[:, mt, cols]
                        values = (whs if last_layer else wh)[:, b.par, mt * DIM:(mt + 1) * DIM]
                        last = nc.tensor.matmul(psO[:, t * DIM:(t + 1) * DIM], weights, values,
                                                start=(mt == 0), stop=(mt == TILES - 1))
                last.then_inc(s["pv_done"], 1)

            def step(b0, b1, b2, b3, b4):
                if b1:
                    pe.wait_ge(s["h_ready"], b1.n + 1)
                    if due(b1.n):
                        pe.wait_ge(s["eown_ready"], b1.n)
                    for t in range(TILES):
                        last = nc.tensor.transpose(psE[:, t * P:(t + 1) * P], h[:, t * DIM:(t + 1) * DIM],
                                                   c["ident"])
                    last.then_inc(s["hT_psum"], 1)
                if b3 and not last_layer:
                    for t in range(TILES):
                        if t < TILES // 2:
                            pe.wait_ge(s["prob_dve"], 2 * b3.n + t + 1)
                        else:
                            pe.wait_ge(s["prob_ready"], 2 * b3.n + t - 1)
                        if due(2 * b3.n + t // 2):
                            pe.wait_ge(s["probT_act" if t % 2 == 0 else "probT_dve"], 2 * b3.n + t // 2)
                        for mt in range(TILES):
                            last = nc.tensor.transpose(psT[:, t % 2, mt, :], prob[:, b3.par, t, mt * P:(mt + 1) * P],
                                                       c["ident"])
                        last.then_inc(s["probT_psum"], 1)
                if b3 and last_layer:
                    weigh(b3)
                if b1:
                    pe.wait_ge(s["hT_ready"], b1.n + 1)
                    for t in range(TILES):
                        last = nc.tensor.matmul(psE[:, t:t + 1], hT[:, t * P:(t + 1) * P], w["u_own"],
                                                start=True, stop=True)
                    last.then_inc(s["eown_psum"], 1)
                    if due(4 * (b1.n - 1)):
                        pe.wait_ge(s["rise_ready"], 4 * (b1.n - 1))
                        pe.wait_ge(s["erow_ready"], b1.n - 1)
                    nc.tensor.matmul(psR[:, b1.par, :], w["u_row"][:], hT[:], start=True, stop=True
                                     ).then_inc(s["erow_psum"], 1)
                    if due(b1.n):
                        pe.wait_ge(s["wh_ready"], b1.n)
                    for t in range(TILES):
                        last = nc.tensor.matmul(psW[:, t * DIM:(t + 1) * DIM], hT[:, t * P:(t + 1) * P], w["W"],
                                                start=True, stop=True)
                    last.then_inc(s["wh_psum"], 1)
                if b3 and not last_layer:
                    weigh(b3)
            over_steps(pe, step)


def layer2(nc, c, X, adj_in, w, codes):
    KINDS = 4
    with ExitStack() as ctx:
        k = Build(nc, ctx, "kinds")
        norm = Norm(k, "norm", c)
        adj = k.sb("adj", [P, 2, TILES * NODES], BF16)
        is_kind = k.sb("is_kind", [P, KINDS - 1, TILES * NODES], U16)
        not_first = k.sb("not_first", [P, 2, TILES * NODES], BF16)
        h_new = k.sb("h_new", [P, ROW])
        h = k.sb("h", [P, 2, ROW])
        hT = k.sb("hT", [P, NODES])
        hhi, hlo = k.sb("hhi", [P, 2, NODES], F32R), k.sb("hlo", [P, 2, NODES], F32R)
        haT = k.sb("haT", [P, NODES])
        ahi, alo = k.sb("ahi", [P, 2, KINDS, NODES], F32R), k.sb("alo", [P, 2, KINDS, NODES], F32R)
        chosen = k.sb("chosen", [P, 2, NODES])
        leaky = k.sb("leaky", [P, 2, NODES])
        alpha = k.sb("alpha", [P, 2, TILES, NODES])
        xb = k.sb("xb", [P, ROW])

        psS = k.ps("psS", [P, KINDS, NODES])
        psA = k.ps("psA", [P, 2, TILES, 2 * P], BF16)
        psH = k.ps("psH", [P, NODES])
        psO = k.ps("psO", [P, NODES])

        adj_got = [k.sem(f"adj_got{i}") for i in range(2)]
        names = ("first_taken h_new_ready adjT_psum adjT_ready not_first_ready kinds_ready h_ready hT_psum hT_ready hhi_ready hlo_ready "
                 "ahi_ready haT_ready alo_ready score_psum score_taken leaky_ready alpha_ready pv_done xb_ready "
                 "x_updated")
        s = {n: k.sem(n) for n in names.split()}
        block = ctx.enter_context(nc.Block())

        @block.gpsimd
        def _(pool):
            def step(b0, b1, b2, b3, b4):
                if b0:
                    norm.on_pool(nc, pool, b0, s["h_new_ready"], b0.n - 1)
                if b0:
                    if due(4 * (b0.n - 1)):
                        pool.wait_ge(s["adjT_psum"], 4 * (b0.n - 1))
                    pool.dma_start(adj[:, b0.par, :].rearrange("p (t m) -> p t m", m=NODES),
                                   adj_in[bass.ds(b0.n, 1), :, :].rearrange("b (t p) m -> p (b t) m", p=P)
                                   ).then_inc(adj_got[b0.par], 16)
                if b1:
                    pool.wait_ge(s["hT_ready"], b1.n + 1)
                    pool.wait_ge(s["hhi_ready"], b1.n + 1)
                    nc.gpsimd.tensor_tensor(hlo[:, b1.par, :], hT[:], hhi[:, b1.par, :].bitcast(F32),
                                            ALU.subtract).then_inc(s["hlo_ready"], 1)
                    for kd in range(KINDS):
                        u = 4 * b1.n + kd
                        read = held(pool, u)
                        if due(read):
                            pool.wait_ge(s["alo_ready"], 1)
                            pool.wait_ge(s["alo_ready"], read)
                        nc.gpsimd.tensor_scalar(haT[:], hT[:], w["a"][:, kd:kd + 1], 1.0, ALU.mult,
                                                ALU.mult).then_inc(s["haT_ready"], 1)
                        pool.wait_ge(s["haT_ready"], u + 1)
                        pool.wait_ge(s["ahi_ready"], u + 1)
                        nc.gpsimd.tensor_tensor(alo[:, b1.par, kd, :], haT[:],
                                                ahi[:, b1.par, kd, :].bitcast(F32),
                                                ALU.subtract).then_inc(s["alo_ready"], 1)
                if b2:
                    if due(b2.n):
                        pool.wait_ge(s["x_updated"], b2.n)
                    nc.gpsimd.tensor_tensor(xb[:], x_rows(X, b2), c["bias2"][:], ALU.add).then_inc(s["xb_ready"], 1)
            over_steps(pool, step)

        @block.vector
        def _(dve):
            def choose(b, t):
                u = 4 * b.n + t
                halves = [slice(i * NODES // 2, (i + 1) * NODES // 2) for i in range(2)]
                cols = [slice(t * NODES + i * NODES // 2, t * NODES + (i + 1) * NODES // 2) for i in range(2)]
                for kind in range(2, KINDS + 1):
                    for i in range(2):
                        there = held(dve, 4 * u + kind)
                        first, behind = held(dve, u + 1), held(dve, 6 * u + 2 * (kind - 3) + i + 1)
                        dve.wait_ge(s["score_psum"], 1)
                        if i == 0:
                            dve.wait_ge(s["score_psum"], there)
                        if kind == 2:
                            dve.wait_ge(s["first_taken"], first)
                        else:
                            dve.wait_ge(s["score_taken"], behind)
                        nc.vector.copy_predicated(chosen[:, t % 2, halves[i]], is_kind[:, kind - 2, cols[i]],
                                                  psS[:, kind - 1, halves[i]]).then_inc(s["score_taken"], 1)
                dve.wait_ge(s["score_taken"], 6 * u + 6)
                if due(u - 1):
                    dve.wait_ge(s["alpha_ready"], u - 1)
                nc.vector.scalar_tensor_tensor(out=leaky[:, t % 2, :], in0=chosen[:, t % 2, :], scalar=SLOPE,
                                               in1=chosen[:, t % 2, :], op0=ALU.mult,
                                               op1=ALU.max).then_inc(s["leaky_ready"], 1)

            def step(b0, b1, b2, b3, b4):
                if b2:
                    dve.wait_ge(s["kinds_ready"], b2.n + 1)
                if b0:
                    norm.on_dve(nc, dve, x_tiles(X, b0), b0)
                if b2:
                    choose(b2, 0)
                if b2:
                    choose(b2, 1)
                if b3:
                    dve.wait_ge(s["pv_done"], b3.n + 1)
                    dve.wait_ge(s["xb_ready"], b3.n + 1)
                    nc.vector.tensor_tensor(x_rows(X, b3), psO[:], xb[:], ALU.add).then_inc(s["x_updated"], 1)
                if b2:
                    choose(b2, 2)
                    choose(b2, 3)
                if b1:
                    code = codes[:, bass.ds(b1.n * (TILES * NODES), TILES * NODES)]
                    dve.wait_ge(s["adjT_ready"], 4 * b1.n + 4)
                    if due(16 * (b1.n - 1)):
                        dve.wait_ge(s["score_psum"], 16 * (b1.n - 1))
                    nc.vector.tensor_scalar(not_first[:, b1.par, :], code, 1.0, -BIG, ALU.not_equal,
                                            ALU.mult).then_inc(s["not_first_ready"], 1)
                    for kind in range(2, KINDS + 1):
                        last = nc.vector.tensor_scalar(is_kind[:, kind - 2, :], code, float(kind), None, ALU.is_equal)
                    last.then_inc(s["kinds_ready"], 1)
            over_steps(dve, step)

        @block.scalar
        def _(act):
            def take_first(b, t):
                u = 4 * b.n + t
                act.wait_ge(s["score_psum"], 4 * u + 1)
                if due(u - 1):
                    act.wait_ge(s["leaky_ready"], u - 1)
                nc.scalar.activation(chosen[:, t % 2, :], psS[:, 0, :], ACT.Copy).then_inc(s["first_taken"], 1)

            def gates(b, t):
                act.wait_ge(s["leaky_ready"], 4 * b.n + t + 1)
                if due(b.n - 1):
                    act.wait_ge(s["pv_done"], b.n - 1)
                nc.scalar.activation(alpha[:, b.par, t, :], leaky[:, t % 2, :], ACT.Sigmoid
                                     ).then_inc(s["alpha_ready"], 1)

            def codes_of(b, t):
                act.wait_ge(s["adjT_psum"], 4 * b.n + t + 1)
                nc.scalar.activation(codes[:, bass.ds((b.n * TILES + t) * NODES, NODES)],
                                     psA[:, t % 2, :, 0:P], ACT.Copy).then_inc(s["adjT_ready"], 1)

            def step(b0, b1, b2, b3, b4):
                if b2:
                    take_first(b2, 0)
                if b1:
                    act.wait_ge(s["hT_psum"], b1.n + 1)
                    if due(4 * b1.n):
                        act.wait_ge(s["haT_ready"], 4 * b1.n)
                    nc.scalar.activation(hT[:], psH[:], ACT.Copy).then_inc(s["hT_ready"], 1)
                    if due(16 * (b1.n - 1)):
                        act.wait_ge(s["score_psum"], 16 * (b1.n - 1))
                    nc.scalar.activation(hhi[:, b1.par, :], psH[:], ACT.Copy).then_inc(s["hhi_ready"], 1)
                    for kd in range(KINDS):
                        nc.scalar.activation(ahi[:, b1.par, kd, :], psH[:], ACT.Copy, scale=w["a"][:, kd:kd + 1]
                                             ).then_inc(s["ahi_ready"], 1)
                if b1:
                    codes_of(b1, 0)
                    codes_of(b1, 1)
                if b2:
                    take_first(b2, 1)
                    gates(b2, 0)
                if b1:
                    if due(b1.n - 1):
                        act.wait_ge(s["pv_done"], b1.n - 1)
                    act.wait_ge(s["h_new_ready"], b1.n + 1)
                    nc.scalar.activation(h[:, b1.par, :], h_new[:], ACT.Copy).then_inc(s["h_ready"], 1)
                if b2:
                    take_first(b2, 2)
                    gates(b2, 1)
                if b1:
                    codes_of(b1, 2)
                    codes_of(b1, 3)
                if b2:
                    take_first(b2, 3)
                    gates(b2, 2)
                if b0:
                    if due(b0.n):
                        act.wait_ge(s["hT_psum"], b0.n)
                        act.wait_ge(s["h_ready"], b0.n)
                    norm.apply(nc, act, h_new, x_tiles(X, b0), b0, ACT.Relu).then_inc(s["h_new_ready"], 1)
                if b2:
                    gates(b2, 3)
            over_steps(act, step)

        @block.tensor
        def _(pe):
            def products(b, t):
                u = 4 * b.n + t
                cols = slice(t * P, (t + 1) * P)
                if t == 0:
                    pe.wait_ge(s["hhi_ready"], b.n + 1)
                    pe.wait_ge(s["hlo_ready"], b.n + 1)
                for kd in range(KINDS):
                    if t == 0:
                        pe.wait_ge(s["ahi_ready"], 4 * b.n + kd + 1)
                        pe.wait_ge(s["alo_ready"], 4 * b.n + kd + 1)
                    if kd == 0:
                        if due(u):
                            pe.wait_ge(s["first_taken"], u)
                    elif due(6 * (u - 1) + 2 * kd):
                        pe.wait_ge(s["score_taken"], 6 * (u - 1) + 2 * kd)
                    hi, lo = hhi[:, b.par, :], hlo[:, b.par, :]
                    nc.tensor.matmul(psS[:, kd, :], ahi[:, b.par, kd, cols], hi, start=True, stop=False)
                    nc.tensor.matmul(psS[:, kd, :], ahi[:, b.par, kd, cols], lo, start=False, stop=False)
                    last = nc.tensor.matmul(psS[:, kd, :], alo[:, b.par, kd, cols], hi, start=False, stop=kd > 0)
                    if kd == 0:
                        pe.wait_ge(s["not_first_ready"], b.n + 1)
                        last = nc.tensor.matmul(psS[:, kd, :], c["ident_bf"][:],
                                                not_first[:, b.par, t * NODES:(t + 1) * NODES], start=False, stop=True)
                    last.then_inc(s["score_psum"], 1)

            def transpose_codes(b, t):
                if t == 0:
                    pe.wait_ge(adj_got[b.par], 16 * (b.pair + 1))
                if due(4 * b.n + t - 1):
                    pe.wait_ge(s["adjT_ready"], 4 * b.n + t - 1)
                for nt in range(TILES):
                    last = nc.tensor.transpose(psA[:, t % 2, nt, 0:P],
                                               adj[:, b.par, nt * NODES + t * P:nt * NODES + (t + 1) * P],
                                               c["ident_bf"][:])
                last.then_inc(s["adjT_psum"], 1)

            def weigh(b):
                if due(b.n):
                    pe.wait_ge(s["x_updated"], b.n)
                pe.wait_ge(s["alpha_ready"], 4 * b.n + 4)
                pe.wait_ge(s["h_ready"], b.n + 1)
                for t in range(TILES):
                    for mt in range(TILES):
                        last = nc.tensor.matmul(psO[:, t * DIM:(t + 1) * DIM],
                                                alpha[:, b.par, mt, t * P:(t + 1) * P],
                                                h[:, b.par, mt * DIM:(mt + 1) * DIM],
                                                start=(mt == 0), stop=(mt == TILES - 1))
                last.then_inc(s["pv_done"], 1)

            def step(b0, b1, b2, b3, b4):
                if b1:
                    pe.wait_ge(s["h_new_ready"], b1.n + 1)
                    if due(4 * b1.n):
                        pe.wait_ge(s["ahi_ready"], 4 * b1.n)
                    for t in range(TILES):
                        last = nc.tensor.transpose(psH[:, t * P:(t + 1) * P], h_new[:, t * DIM:(t + 1) * DIM],
                                                   c["ident"])
                    last.then_inc(s["hT_psum"], 1)
                if b2:
                    products(b2, 0)
                if b1:
                    transpose_codes(b1, 0)
                    transpose_codes(b1, 1)
                if b3:
                    weigh(b3)
                if b2:
                    products(b2, 1)
                    products(b2, 2)
                if b1:
                    transpose_codes(b1, 2)
                    transpose_codes(b1, 3)
                if b2:
                    products(b2, 3)
            over_steps(pe, step)


FIRST = (("w1T", DIM), ("a1", 2), ("w3T", DIM), ("a3", 2), ("wqT", DIM), ("bq", 1))
KEPT = (("ident", P), ("wkT", DIM), ("wvT", DIM), ("woT", DIM), ("w1", DIM), ("w3", DIM), ("a2", 4), ("bk", 1))


def columns(array, names):
    start = 0
    for name, width in names:
        yield name, array[:, start:start + width]
        start += width


def build(nc, t):
    with ExitStack() as ctx:
        k = Build(nc, ctx, "all")
        X = k.sb("x", [P, BATCH * ROW])
        c = {"ident_bf": k.sb("ident_bf", [P, P], BF16), "bias2": k.sb("bias2", [P, ROW]),
             "minus_half": k.sb("minus_half", [P, TILES])}
        kept = k.sb("kept", t["kept"].shape)
        parts = dict(columns(kept, KEPT))
        c["ident"] = parts["ident"]
        w0 = {"wkT": parts["wkT"], "wvT": parts["wvT"], "woT": parts["woT"], "bk": parts["bk"],
              "wqT": k.sb("wqT", [P, DIM]), "bqs": k.sb("bqs", [P, 1])}
        w1, w2, w3 = {"W": parts["w1"]}, {"a": parts["a2"]}, {"W": parts["w3"]}
        for name, w in (("u1", w1), ("u3", w3)):
            w["u"] = k.sb(name, [P, 2])
            w["u_row"] = k.sb(f"{name}_row", [P, P])
        w1["u_own"], w3["u_own"] = w1["u"][:, 0:1], w3["u"][:, 1:2]

        with ExitStack() as setup:
            kk = Build(nc, setup, "setup")
            ones = kk.sb("ones", [P, P])
            first = kk.sb("first", t["first"].shape)
            once = dict(columns(first, FIRST))
            loads = ((first, t["first"]), (kept, t["kept"]), (c["ident_bf"], t["ident_bf"]), (c["bias2"], t["bias2"]))
            psU = kk.ps("psU", [P, 4])
            got, u_psum, u_ready, ones_ready = kk.sem("got"), kk.sem("u_psum"), kk.sem("u_ready"), kk.sem("ones_ready")
            block = setup.enter_context(nc.Block())

            @block.sync
            def _(sp):
                for dst, src in loads:
                    sp.dma_start(dst[:], src).then_inc(got, 16)

            @block.tensor
            def _(pe):
                pe.wait_ge(got, 16 * len(loads))
                nc.tensor.matmul(psU[:, 0:2], once["w1T"], once["a1"], start=True, stop=True).then_inc(u_psum, 1)
                nc.tensor.matmul(psU[:, 2:4], once["w3T"], once["a3"], start=True, stop=True).then_inc(u_psum, 1)

            @block.vector
            def _(dve):
                nc.vector.memset(c["minus_half"][:], -0.5)
                nc.vector.memset(ones[:], 1.0).then_inc(ones_ready, 1)
                dve.wait_ge(got, 16 * len(loads))
                scale = -float(HDIM) ** -0.5
                nc.vector.tensor_scalar(w0["wqT"][:], once["wqT"], scale, None, ALU.mult)
                nc.vector.tensor_scalar(w0["bqs"][:], once["bq"], scale, None, ALU.mult)
                dve.wait_ge(u_psum, 2)
                nc.vector.tensor_copy(w1["u"][:], psU[:, 0:2]).then_inc(u_ready, 1)
                nc.vector.tensor_copy(w3["u"][:], psU[:, 2:4]).then_inc(u_ready, 1)
                dve.wait_ge(u_ready, 2)
                dve.wait_ge(ones_ready, 1)
                nc.vector.tensor_scalar(w1["u_row"][:], ones[:], w1["u"][:, 1:2], None, ALU.mult)
                nc.vector.tensor_scalar(w3["u_row"][:], ones[:], w3["u"][:, 0:1], None, ALU.mult)

        layer0(nc, c, X, t, w0)
        graph_attention(nc, c, X, t["adj"], w1, None, None, False)
        with nc.sbuf_tensor("codes", [P, BATCH * TILES * NODES], BF16) as codes:
            layer2(nc, c, X, t["adj"], w2, codes)
            graph_attention(nc, c, X, None, w3, codes, t["out"], True)


def kernel(**inputs):
    import concourse.bacc as bacc
    from concourse.bass_utils import run_bass_kernel_spmd

    f = {n: np.ascontiguousarray(a) for n, a in inputs.items()}

    def rows(v):
        return np.ascontiguousarray(np.broadcast_to(np.tile(v, TILES), (P, ROW)))

    parts = {
        "ident": np.eye(P, dtype=np.float32),
        "wqT": f["L0_gnn_Wq"].T, "wkT": f["L0_gnn_Wk"].T, "wvT": f["L0_gnn_Wv"].T, "woT": f["L0_gnn_Wo"].T,
        "bq": f["L0_gnn_bq"][:, None], "bk": f["L0_gnn_bk"][:, None],
        "w1": f["L1_gnn_W"], "w1T": f["L1_gnn_W"].T, "a1": f["L1_gnn_a"].reshape(2, DIM).T,
        "a2": np.concatenate([f[f"L2_gnn_a{i}"] for i in range(4)], axis=1),
        "w3": f["L3_gnn_W"], "w3T": f["L3_gnn_W"].T, "a3": f["L3_gnn_a"].reshape(2, DIM).T,
    }
    arrays = {
        "x": f["x"], "adj": f["adj"], "ident_bf": np.eye(P, dtype=np.float32).astype(mybir.dt.np(BF16)),
        "first": np.concatenate([parts[name] for name, _ in FIRST], axis=1),
        "kept": np.concatenate([parts[name] for name, _ in KEPT], axis=1),
        "rows": np.concatenate([rows(f[f"L0_gnn_{n}"]) for n in ("bv", "bo", "gamma", "beta")], axis=1),
        "bias2": rows(f["L2_gnn_bias"]),
    }
    arrays = {n: np.ascontiguousarray(a) for n, a in arrays.items()}
    nc = bacc.Bacc("TRN2", target_bir_lowering=False, num_devices=1)
    t = {n: nc.dram_tensor(f"in_{n}", a.shape, mybir.dt.from_np(a.dtype), kind="ExternalInput").ap()
         for n, a in arrays.items()}
    t["out"] = nc.dram_tensor("out", (BATCH, NODES, DIM), F32, kind="ExternalOutput").ap()
    build(nc, t)
    r = run_bass_kernel_spmd(nc, [{f"in_{n}": a for n, a in arrays.items()}], core_ids=[0])
    return r.results[0]["out"]
```
